# Optimizing a Trainium2 kernel written in Bass

```python
import numpy as np
import jax
import jax.numpy as jnp

def _softmax(x, axis=-1):
    return jax.nn.softmax(x, axis=axis)

def _gelu(x):
    return jax.nn.gelu(x, approximate=True)

def _silu(x):
    return jax.nn.silu(x)

def _sigmoid(x):
    return jax.nn.sigmoid(x)

def _layernorm(x, axis=-1, eps=1e-05):
    m = jnp.mean(x, axis=axis, keepdims=True)
    v = jnp.var(x, axis=axis, keepdims=True)
    return (x - m) / jnp.sqrt(v + eps)

def _scatter_add(tgt, idx, src, axis=0):
    return tgt.at[idx].add(src)

def _segment_sum(src, seg, n):
    return jax.ops.segment_sum(src, seg, n)
kernel_name = 'mk_decoder_preln_d1_seqx_r8_37487c'

def setup_inputs(seed: int=0):
    np.random.seed(seed)
    _w = jnp.asarray

    def _rec_inputs():
        import jax
        import jax.numpy as jnp
        _rk = jax.random.key(seed)
        x = -0.0002928 + 1 * jax.random.normal(jax.random.fold_in(_rk, 1), (16, 128, 128), jnp.float32)
        _lenS = 128 - jax.random.randint(jax.random.fold_in(_rk, 7), (16,), 0, max(1, 128 // 4) + 1, jnp.int32)
        _lenS2 = 128 - jax.random.randint(jax.random.fold_in(_rk, 8), (16,), 0, max(1, 128 // 4) + 1, jnp.int32)
        _ctx_1024P = jax.random.normal(jax.random.fold_in(_rk, 11), (16, 16, 128), jnp.float32)
        _ctx_1024c = jax.random.dirichlet(jax.random.fold_in(_rk, 511), 0.3 * jnp.ones((16,), jnp.float32), (16, 128))
        _ctx_1024t = jnp.einsum('bsk,bkd->bsd', _ctx_1024c, _ctx_1024P)
        _ctx_1024t = _ctx_1024t * jax.lax.rsqrt(jnp.mean(jnp.square(_ctx_1024t)) + 1e-12) * 0.953939
        ctx_1024 = 4.13588e-05 + 0.999923 * (_ctx_1024t + 0.3 * jax.random.normal(jax.random.fold_in(_rk, 611), (16, 128, 128), jnp.float32))
        fside_Bx16xSxS2_0 = -6.00028e-05 + 1.00001 * jax.random.normal(jax.random.fold_in(_rk, 12), (16, 16, 128, 128), jnp.float32)
        return (x, ctx_1024, fside_Bx16xSxS2_0)
    x, ctx_1024, fside_Bx16xSxS2_0 = _rec_inputs()

    def _L0_attn_setup():
        import jax, jax.numpy as jnp
        import numpy as np
        D_MODEL = 128
        N_HEAD = 16
        SEQ = 256
        BATCH = 2
        key = jax.random.key(seed)
        x = jax.random.normal(key, (BATCH, SEQ, D_MODEL), dtype=jnp.float32)
        return {'x': x}
    _L0_attn_all = _L0_attn_setup()
    _L0_attn_in = {k: v for k, v in _L0_attn_all.items() if k in ()}
    del _L0_attn_all

    def _L0_xattn_setup():
        import jax, jax.numpy as jnp
        import numpy as np
        EMBED_DIM = 128
        NUM_HEADS = 16
        HEAD_DIM = EMBED_DIM // NUM_HEADS
        BSZ, TGT, SRC = (4, 128, 256)
        key = jax.random.key(seed)
        ks = jax.random.split(key, 12)
        init = 1.0 / np.sqrt(EMBED_DIM)
        return {'hidden_states': jax.random.normal(ks[0], (BSZ, TGT, EMBED_DIM), jnp.float32), 'key_value_states': jax.random.normal(ks[1], (BSZ, SRC, EMBED_DIM), jnp.float32), 'bias': jax.random.normal(ks[2], (BSZ, NUM_HEADS, TGT, SRC), jnp.float32), 'Wq': jax.random.normal(ks[3], (EMBED_DIM, EMBED_DIM), jnp.float32) * init, 'bq': jax.random.normal(ks[4], (EMBED_DIM,), jnp.float32) * init, 'Wk': jax.random.normal(ks[5], (EMBED_DIM, EMBED_DIM), jnp.float32) * init, 'bk': jax.random.normal(ks[6], (EMBED_DIM,), jnp.float32) * init, 'Wv': jax.random.normal(ks[7], (EMBED_DIM, EMBED_DIM), jnp.float32) * init, 'bv': jax.random.normal(ks[8], (EMBED_DIM,), jnp.float32) * init, 'Wo': jax.random.normal(ks[9], (EMBED_DIM, EMBED_DIM), jnp.float32) * init, 'bo': jax.random.normal(ks[10], (EMBED_DIM,), jnp.float32) * init}
    _L0_xattn_all = _L0_xattn_setup()
    _L0_xattn_in = {k: v for k, v in _L0_xattn_all.items() if k in ('Wq', 'bq', 'Wk', 'bk', 'Wv', 'bv', 'Wo', 'bo')}
    del _L0_xattn_all

    def _L0_ffn_setup():
        import jax, jax.numpy as jnp
        import numpy as np
        B, S, H, NH, E, F = (4, 128, 128, 16, 8, 512)
        D = H // NH
        EPS = 1e-05

        def _layernorm(x, g, b):
            mu = jnp.mean(x, axis=-1, keepdims=True)
            var = jnp.var(x, axis=-1, keepdims=True)
            return (x - mu) * jax.lax.rsqrt(var + EPS) * g + b
        key = jax.random.key(seed)
        ks = jax.random.split(key, 16)
        s = 0.02
        return {'x': jax.random.normal(ks[0], (B, S, H), jnp.float32), 'ln1_g': jnp.ones((H,), jnp.float32), 'ln1_b': jnp.zeros((H,), jnp.float32), 'ln2_g': jnp.ones((H,), jnp.float32), 'ln2_b': jnp.zeros((H,), jnp.float32), 'wq': jax.random.normal(ks[1], (H, H), jnp.float32) * s, 'bq': jnp.zeros((H,), jnp.float32), 'wk': jax.random.normal(ks[2], (H, H), jnp.float32) * s, 'bk': jnp.zeros((H,), jnp.float32), 'wv': jax.random.normal(ks[3], (H, H), jnp.float32) * s, 'bv': jnp.zeros((H,), jnp.float32), 'wo': jax.random.normal(ks[4], (H, H), jnp.float32) * s, 'bo': jnp.zeros((H,), jnp.float32), 'gate_w': jax.random.normal(ks[5], (H, E), jnp.float32) * s, 'gate_b': jnp.zeros((E,), jnp.float32), 'w1': jax.random.normal(ks[6], (E, H, F), jnp.float32) * s, 'b1': jnp.zeros((E, F), jnp.float32), 'w2': jax.random.normal(ks[7], (E, F, H), jnp.float32) * s, 'b2': jnp.zeros((E, H), jnp.float32)}
    _L0_ffn_all = _L0_ffn_setup()
    _L0_ffn_in = {k: v for k, v in _L0_ffn_all.items() if k in ('ln1_g', 'ln1_b', 'ln2_g', 'ln2_b', 'wq', 'bq', 'wk', 'bk', 'wv', 'bv', 'wo', 'bo', 'gate_w', 'gate_b', 'w1', 'b1', 'w2', 'b2')}
    del _L0_ffn_all
    return {'x': x, 'ctx_1024': ctx_1024, 'fside_Bx16xSxS2_0': fside_Bx16xSxS2_0, 'L0_xattn_Wq': _L0_xattn_in['Wq'], 'L0_xattn_bq': _L0_xattn_in['bq'], 'L0_xattn_Wk': _L0_xattn_in['Wk'], 'L0_xattn_bk': _L0_xattn_in['bk'], 'L0_xattn_Wv': _L0_xattn_in['Wv'], 'L0_xattn_bv': _L0_xattn_in['bv'], 'L0_xattn_Wo': _L0_xattn_in['Wo'], 'L0_xattn_bo': _L0_xattn_in['bo'], 'L0_ffn_ln1_g': _L0_ffn_in['ln1_g'], 'L0_ffn_ln1_b': _L0_ffn_in['ln1_b'], 'L0_ffn_ln2_g': _L0_ffn_in['ln2_g'], 'L0_ffn_ln2_b': _L0_ffn_in['ln2_b'], 'L0_ffn_wq': _L0_ffn_in['wq'], 'L0_ffn_bq': _L0_ffn_in['bq'], 'L0_ffn_wk': _L0_ffn_in['wk'], 'L0_ffn_bk': _L0_ffn_in['bk'], 'L0_ffn_wv': _L0_ffn_in['wv'], 'L0_ffn_bv': _L0_ffn_in['bv'], 'L0_ffn_wo': _L0_ffn_in['wo'], 'L0_ffn_bo': _L0_ffn_in['bo'], 'L0_ffn_gate_w': _L0_ffn_in['gate_w'], 'L0_ffn_gate_b': _L0_ffn_in['gate_b'], 'L0_ffn_w1': _L0_ffn_in['w1'], 'L0_ffn_b1': _L0_ffn_in['b1'], 'L0_ffn_w2': _L0_ffn_in['w2'], 'L0_ffn_b2': _L0_ffn_in['b2']}

def reference(x, ctx_1024, fside_Bx16xSxS2_0, L0_xattn_Wq, L0_xattn_bq, L0_xattn_Wk, L0_xattn_bk, L0_xattn_Wv, L0_xattn_bv, L0_xattn_Wo, L0_xattn_bo, L0_ffn_ln1_g, L0_ffn_ln1_b, L0_ffn_ln2_g, L0_ffn_ln2_b, L0_ffn_wq, L0_ffn_bq, L0_ffn_wk, L0_ffn_bk, L0_ffn_wv, L0_ffn_bv, L0_ffn_wo, L0_ffn_bo, L0_ffn_gate_w, L0_ffn_gate_b, L0_ffn_w1, L0_ffn_b1, L0_ffn_w2, L0_ffn_b2):
    import jax
    import jax.numpy as jnp

    def _L0_attn_ref(x):
        import jax, jax.numpy as jnp
        import numpy as np
        D_MODEL = 128
        N_HEAD = 16
        SEQ = 256
        BATCH = 2
        B, S, D = x.shape
        H = N_HEAD
        hd = D // H
        qkv = x.reshape(B, S, H, hd).transpose(0, 2, 1, 3)
        q = k = v = qkv
        w = jnp.einsum('bhqd,bhkd->bhqk', q, k) / jnp.sqrt(jnp.asarray(hd, x.dtype))
        causal = jnp.tril(jnp.ones((S, S), dtype=bool))
        mask_value = jnp.finfo(w.dtype).min
        w = jnp.where(causal[None, None, :, :], w, mask_value)
        w = jax.nn.softmax(w, axis=-1)
        out = jnp.einsum('bhqk,bhkd->bhqd', w, v)
        return out.transpose(0, 2, 1, 3).reshape(B, S, D)

    def _L0_xattn_ref(hidden_states, key_value_states, bias, Wq, bq, Wk, bk, Wv, bv, Wo, bo):
        import jax, jax.numpy as jnp
        import numpy as np
        EMBED_DIM = 128
        NUM_HEADS = 16
        HEAD_DIM = EMBED_DIM // NUM_HEADS
        BSZ, TGT, SRC = (4, 128, 256)
        B, T, E = hidden_states.shape
        S = key_value_states.shape[1]
        H, hd = (NUM_HEADS, HEAD_DIM)
        scaling = hd ** (-0.5)
        q = (hidden_states @ Wq.T + bq) * scaling
        k = key_value_states @ Wk.T + bk
        v = key_value_states @ Wv.T + bv
        q = q.reshape(B, T, H, hd).transpose(0, 2, 1, 3)
        k = k.reshape(B, S, H, hd).transpose(0, 2, 1, 3)
        v = v.reshape(B, S, H, hd).transpose(0, 2, 1, 3)
        scores = jnp.einsum('bhtd,bhsd->bhts', q, k) + bias
        probs = jax.nn.softmax(scores, axis=-1)
        attn = jnp.einsum('bhts,bhsd->bhtd', probs, v)
        attn = attn.reshape(B, T, E)
        return attn @ Wo.T + bo

    def _L0_ffn_ref(x, ln1_g, ln1_b, ln2_g, ln2_b, wq, bq, wk, bk, wv, bv, wo, bo, gate_w, gate_b, w1, b1, w2, b2):
        import jax, jax.numpy as jnp
        import numpy as np
        B, S, H, NH, E, F = (4, 128, 128, 16, 8, 512)
        D = H // NH
        EPS = 1e-05

        def _layernorm(x, g, b):
            mu = jnp.mean(x, axis=-1, keepdims=True)
            var = jnp.var(x, axis=-1, keepdims=True)
            return (x - mu) * jax.lax.rsqrt(var + EPS) * g + b
        b, s, h = x.shape
        hn = _layernorm(x, ln1_g, ln1_b)
        q = (hn @ wq + bq).reshape(b, s, NH, D).transpose(0, 2, 1, 3)
        k = (hn @ wk + bk).reshape(b, s, NH, D).transpose(0, 2, 1, 3)
        v = (hn @ wv + bv).reshape(b, s, NH, D).transpose(0, 2, 1, 3)
        scores = jnp.einsum('bhqd,bhkd->bhqk', q, k) / jnp.sqrt(jnp.float32(D))
        attn = jax.nn.softmax(scores, axis=-1)
        o = jnp.einsum('bhqk,bhkd->bhqd', attn, v)
        o = o.transpose(0, 2, 1, 3).reshape(b, s, h)
        x = x + (o @ wo + bo)
        hn2 = _layernorm(x, ln2_g, ln2_b).reshape(-1, h)
        logits = hn2 @ gate_w + gate_b
        idx = jnp.argmax(logits, axis=-1)
        mid = jax.nn.relu(jnp.einsum('th,ehf->etf', hn2, w1) + b1[:, None, :])
        y = jnp.einsum('etf,efh->eth', mid, w2) + b2[:, None, :]
        moe = y[idx, jnp.arange(hn2.shape[0])]
        return x + moe.reshape(b, s, h)
    x = x + _L0_attn_ref(_layernorm(x, axis=-1))
    x = x + _L0_xattn_ref(_layernorm(x, axis=-1), ctx_1024, fside_Bx16xSxS2_0, L0_xattn_Wq, L0_xattn_bq, L0_xattn_Wk, L0_xattn_bk, L0_xattn_Wv, L0_xattn_bv, L0_xattn_Wo, L0_xattn_bo)
    x = x + _L0_ffn_ref(_layernorm(x, axis=-1), L0_ffn_ln1_g, L0_ffn_ln1_b, L0_ffn_ln2_g, L0_ffn_ln2_b, L0_ffn_wq, L0_ffn_bq, L0_ffn_wk, L0_ffn_bk, L0_ffn_wv, L0_ffn_bv, L0_ffn_wo, L0_ffn_bo, L0_ffn_gate_w, L0_ffn_gate_b, L0_ffn_w1, L0_ffn_b1, L0_ffn_w2, L0_ffn_b2)
    return x

_drawn_inputs = setup_inputs


def setup_inputs(seed=0):
    import zlib

    import numpy as np

    out = dict(_drawn_inputs(seed))
    spreads = {'L0_ffn_ln1_g': (1.0, 0.6),
     'L0_ffn_ln1_b': (0.0, 0.8),
     'L0_ffn_ln2_g': (1.0, 0.6),
     'L0_ffn_ln2_b': (0.0, 0.567),
     'L0_ffn_bq': (0.0, 0.8),
     'L0_ffn_bk': (0.0, 2.0),
     'L0_ffn_bv': (0.0, 0.613),
     'L0_ffn_bo': (0.0, 0.278),
     'L0_ffn_gate_b': (0.0, 0.1),
     'L0_ffn_b1': (0.0, 0.707),
     'L0_ffn_b2': (0.0, 0.339)}
    factors = {'L0_xattn_bq': 3.752,
     'L0_xattn_bk': 64.0,
     'L0_ffn_wq': 8.0,
     'L0_ffn_wk': 8.0,
     'L0_ffn_wv': 8.0,
     'L0_ffn_wo': 4.675}
    for name, (base, spread) in spreads.items():
        noise = np.random.default_rng([zlib.crc32(name.encode()), seed]).standard_normal(out[name].shape)
        drawn = base * np.exp(spread * noise) if base else spread * noise
        out[name] = jnp.asarray(drawn.astype(out[name].dtype))
    for name, factor in factors.items():
        out[name] = (out[name] * factor).astype(out[name].dtype)
    return out
```

```python
import numpy as np
from contextlib import ExitStack

import concourse.bass as bass
from concourse import mybir

B, S, D = 16, 128, 128
NH, HD = 16, 8
E, F = 8, 512
FC = F // 128
EPS = 1e-5
SCALE = HD ** -0.5
G = 4
NG = NH // G
PAIR = 2 * S
NPAIR = B // 2
UNROLL = 4
NT = 3
ROWS = NT * NT * HD
KROWS = 96
VC = 32
MASKED = -1e30
TR = D // HD
TQ = S // TR

SELF, CROSS, FFN = 0, 1, 2
PERM_M = NG + 1


def wait(eng, sem, value, apart=None):
    if not isinstance(value, int) or value > 0:
        eng.wait_ge(sem, value)
        if apart is not None and not isinstance(value, int):
            eng.sem_inc(apart, 1)


class Step:

    def __init__(self, eng, layer, t):
        fixed = isinstance(t, int)
        snap = (lambda v: v) if fixed else eng.snap
        self.layer, self.t = layer, t
        self.first = snap(t * UNROLL)
        self.groups = snap(t * (UNROLL * NG))
        self.maxes = snap(t * (UNROLL * PERM_M))

    def batch(self, k):
        return self.first + (B * self.layer + k)

    def group(self, k, g):
        return self.groups + (B * NG * self.layer + k * NG + g)

    def maxuse(self, k, g):
        return self.maxes + (B * PERM_M * (self.layer - 1) + k * PERM_M + g)

    def pair(self, j):
        return self.t * 2 + (NPAIR * self.layer + j)

    def turn(self, j):
        return self.t + (NPAIR // 2 * self.layer + j // 2)


def build(nc, a, out):
    f32, bf16 = mybir.dt.float32, mybir.dt.bfloat16
    ALU, ACT, AX = mybir.AluOpType, mybir.ActivationFunctionType, mybir.AxisListType

    ctx = ExitStack()
    with ctx:
        def sb(name, shape, dt=f32):
            return ctx.enter_context(nc.sbuf_tensor(name, shape, dt))

        def sem(name):
            return ctx.enter_context(nc.semaphore(name))

        x_sb = sb("x_sb", [128, B, D])
        y_sb = sb("y_sb", [128, B, D])
        xn = sb("xn", [128, 2, 2, D])
        stats = sb("stats", [128, 2, 6])
        meanvar = sb("meanvar", [128, 2, 2])
        vareps = sb("vareps", [128, 2])
        rstd = sb("rstd", [128, 2])
        ctx_in = sb("ctx_in", [128, 2, 2, D])
        hT = sb("hT", [128, 2, 2, PAIR])
        qk = sb("qk", [128, 2, PAIR])
        rest = sb("rest", [128, 2, PAIR])
        parts = sb("parts", [128, 2, NT, 2, PAIR], bf16)
        stack = sb("stack", [KROWS, 2, 2, NH, PAIR], bf16)
        vaug = sb("vaug", [128, UNROLL, NH, VC])
        bias_in = sb("bias_in", [128, 4, NH, S])
        probs = sb("probs", [128, NG, G * S])
        rowmax = sb("rowmax", [128, NH])
        maxparts = sb("maxparts", [128, 128], bf16)
        maxT = sb("maxT", [128, 2, 128], bf16)
        outT = sb("outT", [128, 2, NG * S])
        rowsum_inv = sb("rowsum_inv", [128, NH])
        att = sb("att", [128, D])
        attT = sb("attT", [128, S])
        ident = sb("ident", [128, 128])
        identb = sb("identb", [128, 128], bf16)
        causal = sb("causal", [128, S], bf16)
        pick = sb("pick", [128, NH, S], bf16)
        minus_half = sb("minus_half", [128, 2])
        in_block = sb("in_block", [128, TQ])
        inv_sel = sb("inv_sel", [128, NH, TQ])
        att_sel = sb("att_sel", [128, HD, NH, TQ])
        wxo = sb("wxo", [128, HD, D])
        wx = {k: sb("w_" + k, [128, D]) for k in ("xq", "xk", "xv", "fq", "fk", "fv", "fo")}
        cols = sb("cols", [128, 8])
        xbq_scaled = sb("xbq_scaled", [128, 1])
        rows = sb("rows", [128, 4, D])
        gate_w = sb("gate_w", [128, E])
        gate_b = sb("gate_b", [128, E])
        w1 = sb("w1", [128, E, F])
        w2 = sb("w2", [128, E, FC, D])
        b1 = sb("b1", [128, E, FC])
        b2 = sb("b2", [1, E, D])
        ones_row = sb("ones_row", [1, S])
        hn2T = sb("hn2T", [128, B * S])
        logits = sb("logits", [128, B, E])
        best = sb("best", [128, B])
        is_best = sb("is_best", [128, B, E])
        expert_no = sb("expert_no", [128, E])
        place = sb("place", [128, B, E])
        first_best = sb("first_best", [128, B])
        onehot = sb("onehot", [128, B, E])
        mid = sb("mid", [128, 2, FC, S])

        pb = ctx.enter_context(nc.psum_tensor("prep_bank", [128, 512], f32))
        fb = ctx.enter_context(nc.psum_tensor("finish_bank", [128, 512], f32))
        sbk = [ctx.enter_context(nc.psum_tensor(f"score_bank{i}", [128, G * S], f32)) for i in range(2)]
        mbk = [ctx.enter_context(nc.psum_tensor(f"max_bank{i}", [128, G * S], f32)) for i in range(2)]
        obk = [ctx.enter_context(nc.psum_tensor(f"out_bank{i}", [128, NG * S], f32)) for i in range(2)]

        scratch = nc.dram_tensor("parts_scratch", (2, 2, NT, HD, NH, PAIR), bf16, kind="Internal").ap()
        row_elems = NH * PAIR

        WRITES, READS = 2 * NT * 16, (NT + 1) * 16

        s_apart_dve = sem("waited_apart_dve")
        s_apart_pool = sem("waited_apart_pool")
        s_x = sem("x_loaded")
        s_w = sem("weights_loaded")
        s_moe = sem("expert_weights_loaded")
        s_ctx = [sem(f"ctx_loaded{i}") for i in range(2)]
        s_bias = [sem(f"bias_loaded{i}") for i in range(4)]
        s_wr = [sem(f"scratch_written{i}") for i in range(2)]
        s_stack = [sem(f"stack_loaded{i}") for i in range(2)]
        s_out = sem("out_stored")
        s_pool_const = sem("pool_constants")
        s_dve_const = sem("dve_constants")
        s_stats = sem("stats_ready")
        s_mv = sem("meanvar_ready")
        s_ve = sem("vareps_ready")
        s_rstd = sem("rstd_ready")
        s_y = sem("ffn_input_ready")
        s_xn = sem("xn_ready")
        s_t = sem("transposed")
        s_hT = sem("hT_ready")
        s_qkp = sem("qk_products")
        s_qk = sem("qk_ready")
        s_hi = sem("high_parts")
        s_r1 = sem("first_rest")
        s_mid = sem("middle_parts")
        s_lo = sem("low_parts")
        s_resbias = sem("residual_biased")
        s_vp = sem("v_products")
        s_v = sem("v_ready")
        s_mp = sem("max_products")
        s_mfree = sem("max_bank_free")
        s_mhi = sem("max_high_part")
        s_mparts = sem("max_parts")
        s_e = sem("scores_ready")
        s_p = sem("probs_ready")
        s_pv = sem("outputs_added")
        s_oevac = sem("out_copied")
        s_otr = sem("out_transposed")
        s_inv = sem("rowsum_inverted")
        s_invsel = sem("inverse_in_block")
        s_att = sem("attention_ready")
        s_atr = sem("attention_transposed")
        s_attT = sem("attT_ready")
        s_oproj = sem("out_projected")
        s_res = sem("residual_done")
        s_g = sem("gate_products")
        s_hn2 = sem("hn2T_ready")
        s_rr = sem("residuals_summed")
        s_chain = sem("gate_chain")
        s_up = sem("hidden_products")
        s_mid2 = sem("hidden_ready")
        s_dn = sem("expert_output")
        s_acc = sem("expert_added")

        P_CREDIT, PV_CREDIT, OEV_CREDIT, OTR_CREDIT, RES_CREDIT, MFREE_CREDIT = 2, 4, 2, 2, 1, 2
        DN_CREDIT, ACC_CREDIT = 2, 2

        block = ctx.enter_context(nc.Block())

        def steps(eng, layer, slot):
            def body(t, last):
                st = Step(eng, layer, t)
                for k in range(UNROLL):
                    slot(st, k, last)
            with eng.Fori(0, B // UNROLL - 1) as t:
                body(t, False)
            body(B // UNROLL - 1, True)

        @block.sync
        def _(sp):
            xr = a["x"].rearrange("b s d -> s b d")
            sp.dma_start(x_sb[:, 0:4, :], xr[:, 0:4, :]).then_inc(s_x, 16)
            sp.dma_start(x_sb[:, 4:B, :], xr[:, 4:B, :]).then_inc(s_x, 16)
            for k in wx:
                sp.dma_start(wx[k][:], a["w_" + k]).then_inc(s_w, 16)
            sp.dma_start(wxo[:].rearrange("p d n -> p (d n)"),
                         bass.AP(tensor=a["w_xo"].tensor, offset=a["w_xo"].offset,
                                 ap=[[0, TQ], [HD * D, TR], [1, HD * D]])).then_inc(s_w, 16)
            sp.dma_start(cols[:], a["cols"]).then_inc(s_w, 16)
            for i, k in enumerate(("xbv", "xbo", "fbv", "fbo")):
                sp.dma_start(rows[:, i, :], a[k].partition_broadcast(128)).then_inc(s_w, 16)
            sp.dma_start(gate_w[:], a["gate_w"]).then_inc(s_w, 16)
            sp.dma_start(gate_b[:], a["gate_b"].partition_broadcast(128)).then_inc(s_w, 16)

            def write_parts(layer, turn, i, pair_no):
                wait(sp, s_lo, pair_no + 1)
                wait(sp, s_stack[i], turn * READS)
                for w in range(1 if layer == SELF else 2):
                    for part in range(NT):
                        sp.dma_start(scratch[i, w, part].rearrange("d h k -> h d k"),
                                     parts[:, i, part, w, :]).then_inc(s_wr[i], 16)
                if layer == SELF:
                    sp.sem_inc(s_wr[i], WRITES // 2)

            def read_stack(layer, turn, i, pair_no):
                wait(sp, s_wr[i], turn * WRITES + WRITES)
                wait(sp, s_e, pair_no * (2 * NG) - 2 * (2 * NG) + 2 * NG)
                wk = 0 if layer == SELF else 1
                for part in range(NT):
                    q_src = bass.AP(tensor=scratch.tensor, offset=scratch[i, 0, part].offset,
                                    ap=[[0, NT], [row_elems, HD], [1, row_elems]])
                    r0 = part * NT * HD
                    sp.dma_start(stack[r0:r0 + NT * HD, i, 0, :, :], q_src).then_inc(s_stack[i], 16)
                k_src = bass.AP(tensor=scratch.tensor, offset=scratch[i, wk].offset,
                                ap=[[0, NT], [row_elems, NT * HD], [1, row_elems]])
                sp.dma_start(stack[0:ROWS, i, 1, :, :], k_src).then_inc(s_stack[i], 16)

            def load_bias(n, batch_no, i, turn):
                wait(sp, s_e, (batch_no - 3) * NG)
                src = a["bias"][bass.ds(n, 1)].rearrange("o h q k -> q (o h) k")
                for g in range(NG):
                    sp.dma_start(bias_in[:, i, g * G:(g + 1) * G, :],
                                 src[:, g * G:(g + 1) * G, :]).then_inc(s_bias[i], 16)

            def load_ctx(first, i, pair_no):
                wait(sp, s_t, pair_no - 1)
                sp.dma_start(ctx_in[:, i, :, :],
                             a["ctx"][bass.ds(first, 2)].rearrange("b s d -> s b d")).then_inc(s_ctx[i], 16)

            sp.wait_ge(s_dve_const, 1)
            for layer in (SELF, CROSS, FFN):
                z = Step(sp, layer, 0)
                if layer == CROSS:
                    for n in range(3):
                        load_bias(n, z.batch(n), n, 0)
                    for j in range(2):
                        load_ctx(2 * j, j, z.pair(j))
                if layer == SELF:
                    sp.dma_start(w1[:], a["w1"].rearrange("e h f -> h e f")).then_inc(s_moe, 16)
                    sp.dma_start(w2[:], a["w2"].rearrange("e (c p) h -> p e c h", p=128)).then_inc(s_moe, 16)
                    sp.dma_start(b1[:], a["b1"]).then_inc(s_moe, 16)
                    sp.dma_start(b2[:], a["b2"]).then_inc(s_moe, 16)
                write_parts(layer, z.turn(0), 0, z.pair(0))
                read_stack(layer, z.turn(0), 0, z.pair(0))
                write_parts(layer, z.turn(1), 1, z.pair(1))

                def slot(st, k, last):
                    j = k // 2
                    if layer == CROSS and not (last and k >= 1):
                        load_bias(st.first + (k + 3), st.batch(k + 3), (k + 3) % 4, 0)
                    if k % 2 == 0:
                        if not (last and j == 1):
                            read_stack(layer, st.turn(j + 1), (j + 1) % 2, st.pair(j + 1))
                        if not last:
                            if layer == CROSS:
                                load_ctx(st.first + 2 * (j + 2), j, st.pair(j + 2))
                            write_parts(layer, st.turn(j + 2), j, st.pair(j + 2))

                steps(sp, layer, slot)

            outr = out.rearrange("b s d -> s b d")
            with sp.Fori(0, B // 2) as t:
                sp.wait_ge(s_acc, t * (2 * E) + (2 * E + ACC_CREDIT))
                sp.dma_start(outr[:, bass.ds(t * 2, 2), :], x_sb[:, bass.ds(t * 2, 2), :]).then_inc(s_out, 16)
            sp.wait_ge(s_out, 16 * (B // 2))

        @block.gpsimd
        def _(pool):
            nc.gpsimd.memset(ident[:], 0.0).then_inc(s_pool_const, 1)
            nc.gpsimd.memset(minus_half[:], -0.5).then_inc(s_pool_const, 1)
            nc.gpsimd.memset(causal[:], 0.0).then_inc(s_pool_const, 1)
            nc.gpsimd.memset(pick[:], 0.0).then_inc(s_pool_const, 1)
            nc.gpsimd.memset(in_block[:], 1.0).then_inc(s_pool_const, 1)
            pool.wait_ge(s_pool_const, 5)
            nc.gpsimd.affine_select(out=ident[:], in_=ident[:], compare_op=ALU.not_equal, fill=1.0, base=0,
                                    pattern=[[-1, 128]], channel_multiplier=1).then_inc(s_pool_const, 1)
            nc.gpsimd.affine_select(out=causal[:], in_=causal[:], compare_op=ALU.is_ge, fill=MASKED, base=0,
                                    pattern=[[1, S]], channel_multiplier=-1).then_inc(s_pool_const, 1)
            nc.gpsimd.affine_select(out=pick[:], in_=pick[:], compare_op=ALU.not_equal, fill=1.0, base=0,
                                    pattern=[[-1, NH], [0, S]], channel_multiplier=1).then_inc(s_pool_const, 1)
            nc.gpsimd.affine_select(out=in_block[:], in_=in_block[:], compare_op=ALU.is_ge, fill=0.0, base=0,
                                    pattern=[[-TR, TQ]], channel_multiplier=1).then_inc(s_pool_const, 1)
            pool.wait_ge(s_pool_const, 9)
            nc.gpsimd.affine_select(out=in_block[:], in_=in_block[:], compare_op=ALU.is_ge, fill=0.0, base=TR - 1,
                                    pattern=[[TR, TQ]], channel_multiplier=-1).then_inc(s_pool_const, 1)
            nc.gpsimd.affine_select(out=pick[:], in_=pick[:], compare_op=ALU.not_equal, fill=1.0, base=-NH,
                                    pattern=[[-1, NH], [0, S]], channel_multiplier=1).then_inc(s_pool_const, 1)
            nc.gpsimd.iota(expert_no[:], pattern=[[1, E]], base=0, channel_multiplier=0,
                           allow_small_or_imprecise_dtypes=True).then_inc(s_pool_const, 1)
            pool.wait_ge(s_w, 16 * 15)

            def inverse_deviation(norm_no):
                wait(pool, s_mv, norm_no * 2 + 2, s_apart_pool)
                nc.gpsimd.tensor_scalar(vareps[:], meanvar[:, :, 1], EPS, None, ALU.add).then_inc(s_ve, 1)
                wait(pool, s_ve, norm_no + 1)
                nc.gpsimd.tensor_tensor(rstd[:], vareps[:], minus_half[:], ALU.pow).then_inc(s_rstd, 1)

            def norm_no(st, j):
                return st.pair(j) if st.layer < FFN else (st.t * 4 + (2 * NPAIR + 2 * j))

            def start_pair(st, j):
                inverse_deviation(norm_no(st, j))
                if st.layer == FFN:
                    inverse_deviation(norm_no(st, j) + 1)
                if st.layer != SELF:
                    wait(pool, s_xn, st.pair(j) * 2 + 2)
                    res = x_sb if st.layer == CROSS else y_sb
                    row = rows[:, 1 if st.layer == CROSS else 3, :]
                    for s in range(2):
                        r = res[:, st.first + (2 * j + s), :]
                        last = nc.gpsimd.tensor_tensor(r, r, row, ALU.add)
                    last.then_inc(s_resbias, 1)

            def low_parts(st, j):
                i = j % 2
                n = 1 if st.layer == SELF else 2
                wait(pool, s_mid, st.pair(j) + 1)
                nc.gpsimd.tensor_tensor(parts[:, i, 2, 0:n, :], rest[:, 0:n, :], parts[:, i, 1, 0:n, :],
                                        ALU.subtract).then_inc(s_lo, 1)

            def self_values(st, j):
                wait(pool, s_xn, st.pair(j) * 2 + 2)
                for s in range(2):
                    wait(pool, s_pv, (st.pair(j) * 2 - 2) * NG + PV_CREDIT, s_apart_pool)
                    nc.gpsimd.tensor_copy(vaug[:, (2 * j + s) % UNROLL, :, 0:HD],
                                          xn[:, j % 2, s, :].rearrange("p (h d) -> p h d", d=HD)).then_inc(s_v, 1)

            pool.wait_ge(s_dve_const, 2)
            for layer in (SELF, CROSS, FFN):
                z = Step(pool, layer, 0)
                start_pair(z, 0)
                low_parts(z, 0)
                if layer == SELF:
                    self_values(z, 0)
                start_pair(z, 1)
                low_parts(z, 1)

                def slot(st, k, last):
                    j = k // 2
                    if k % 2 == 0 and not last:
                        start_pair(st, j + 2)
                    if k % 2 == 1:
                        if layer == SELF and not (last and j == 1):
                            self_values(st, j + 1)
                        if not last:
                            low_parts(st, j + 2)

                steps(pool, layer, slot)

            with pool.Fori(0, NPAIR) as t:
                inverse_deviation(t + 4 * NPAIR)
                pool.wait_ge(s_hn2, t + 1)
                last = nc.gpsimd.tensor_tensor(x_sb[:, bass.ds(t * 2, 2), :], x_sb[:, bass.ds(t * 2, 2), :],
                                               y_sb[:, bass.ds(t * 2, 2), :], ALU.add).then_inc(s_rr, 1)

        @block.tensor
        def _(pe):
            def mm(o, lhsT, rhs, start=True, stop=True, **kw):
                return nc.tensor.matmul(o, lhsT, rhs, start=start, stop=stop, **kw)

            def tr(o, src, stop=True):
                return nc.tensor.matmul(o, src, ident[:], start=True, stop=stop, is_transpose=True)

            def transposes(st, j):
                i = j % 2
                wait(pe, s_xn, st.pair(j) * 2 + 2)
                if st.layer == SELF:
                    wait(pe, s_r1, st.pair(j))
                elif st.layer == CROSS:
                    wait(pe, s_ctx[i], st.t * 16 + (j // 2 * 16 + 16))
                for s in range(2):
                    last = tr(pb[:, s * S:(s + 1) * S], xn[:, i, s, :])
                if st.layer == CROSS:
                    for s in range(2):
                        last = tr(pb[:, PAIR + s * S:PAIR + (s + 1) * S], ctx_in[:, i, s, :])
                last.then_inc(s_t, 1)

            def qk_products(st, j):
                i, key_side = j % 2, 1 if st.layer == CROSS else 0
                wq, wk = ("xq", "xk") if st.layer == CROSS else ("fq", "fk")
                wait(pe, s_hT, st.pair(j) + 1 - NPAIR)
                mm(pb[:, 0:PAIR], wx[wq][:], hT[:, i, 0, :])
                mm(pb[:, PAIR:2 * PAIR], wx[wk][:], hT[:, i, key_side, :]).then_inc(s_qkp, 1)

            def v_products(st, j):
                i, key_side = j % 2, 1 if st.layer == CROSS else 0
                wv = wx["xv" if st.layer == CROSS else "fv"]
                for s in range(2):
                    last = mm(pb[:, s * S:(s + 1) * S], hT[:, i, key_side, s * S:(s + 1) * S], wv[:])
                last.then_inc(s_vp, 1)

            def score_maxes(st, k, g):
                wait(pe, s_mfree, st.maxuse(k, g) + (1 - 2 + MFREE_CREDIT))
                if g == 0:
                    wait(pe, s_stack[k // 2 % 2], st.turn(k // 2) * READS + READS)
                i, s, bank = k // 2 % 2, k % 2, mbk[(k * PERM_M + g) % 2]
                for h in range(G):
                    last = mm(bank[:, h * S:(h + 1) * S],
                              stack[:, i, 0, g * G + h, s * S:(s + 1) * S], stack[:, i, 1, g * G + h, s * S:(s + 1) * S])
                last.then_inc(s_mp, 1)

            def max_transposed(st, k):
                wait(pe, s_mparts, st.batch(k) + (1 - B))
                wait(pe, s_mfree, st.maxuse(k, NG) + (1 - 2 + MFREE_CREDIT))
                bank = mbk[(k * PERM_M + NG) % 2]
                nc.tensor.transpose(bank[:].bitcast(bf16)[:, 0:128], maxparts[:], identb[:]).then_inc(s_mp, 1)

            def scores(st, k, g):
                i, s, bank = k // 2 % 2, k % 2, sbk[g % 2]
                wait(pe, s_p, st.group(k, g) + (1 - 2 + P_CREDIT))
                if g == 0:
                    wait(pe, s_stack[i], st.turn(k // 2) * READS + READS)
                    if st.layer == CROSS:
                        wait(pe, s_bias[k % 4], st.t * (16 * NG) + 16 * NG)
                    if st.layer != SELF:
                        wait(pe, s_mfree, st.maxuse(k, NG) + (1 + MFREE_CREDIT))
                for h in range(G):
                    o, head = bank[:, h * S:(h + 1) * S], g * G + h
                    q = stack[:, i, 0, head, s * S:(s + 1) * S]
                    key = stack[:, i, 1, head, s * S:(s + 1) * S]
                    if st.layer == SELF:
                        mm(o, identb[:], causal[:], stop=False)
                    elif st.layer == CROSS:
                        tr(o, bias_in[:, k % 4, head, :], stop=False)
                    last = mm(o, key, q, start=st.layer == FFN, stop=st.layer == SELF)
                    if st.layer != SELF:
                        last = mm(o, pick[:, head, :], maxT[:, k % 2, :], start=False)
                last.then_inc(s_e, 1)

            def add_outputs(st, k, g):
                wait(pe, s_p, st.group(k, g) + (1 + P_CREDIT))
                if g == 0:
                    wait(pe, s_v, st.batch(k) + (2 - k % 2))
                    wait(pe, s_oevac, st.batch(k) + (1 - 2 + OEV_CREDIT))
                for h in range(G):
                    last = mm(obk[k % 2][VC * h:VC * (h + 1), g * S:(g + 1) * S], vaug[:, k, g * G + h, :],
                              probs[:, g, h * S:(h + 1) * S], tile_position=(0, VC * h))
                last.then_inc(s_pv, 1)

            def out_transposed(st, k):
                wait(pe, s_oevac, st.batch(k) + (1 + OEV_CREDIT))
                wait(pe, s_res, st.batch(k) + (1 - 1 + RES_CREDIT))
                for g in range(NG):
                    last = tr(fb[:, g * S:(g + 1) * S], outT[:, k % 2, g * S:(g + 1) * S])
                last.then_inc(s_otr, 1)

            def attention_transposed(st, k):
                wait(pe, s_att, st.batch(k) + 1)
                tr(fb[:, 0:S], att[:]).then_inc(s_atr, 1)

            def out_projected(st, k):
                if st.layer == CROSS:
                    wait(pe, s_att, st.batch(k) + 1)
                    for d in range(HD):
                        last = mm(fb[:, 0:D], att_sel[:, d, :, :].rearrange("p h t -> p (h t)"), wxo[:, d, :],
                                  start=d == 0, stop=d == HD - 1)
                    last.then_inc(s_oproj, 1)
                else:
                    wait(pe, s_attT, st.batch(k) + (1 - 2 * B))
                    mm(fb[:, 0:D], attT[:], wx["fo"][:]).then_inc(s_oproj, 1)

            pe.sem_inc(s_pv, PV_CREDIT)
            pe.sem_inc(s_otr, OTR_CREDIT)
            pe.sem_inc(s_dn, DN_CREDIT)
            pe.wait_ge(s_pool_const, 12)
            pe.wait_ge(s_dve_const, 4)
            pe.wait_ge(s_w, 16 * 15)
            for layer in (SELF, CROSS, FFN):
                z = Step(pe, layer, 0)
                full = layer != SELF
                for j in range(2):
                    if layer == CROSS and j == 0:
                        pe.wait_ge(s_r1, NPAIR)
                    if layer == FFN and j == 0:
                        pe.wait_ge(s_v, 2 * B)
                    if full and j == 1:
                        wait(pe, s_v, z.batch(2))
                    transposes(z, j)
                    if full:
                        qk_products(z, j)
                        wait(pe, s_qk, z.pair(j) + 1 - NPAIR)
                    if full and j == 0:
                        v_products(z, 0)
                if full:
                    for g in range(NG):
                        score_maxes(z, 0, g)
                    max_transposed(z, 0)

                def slot(st, k, last):
                    j = k // 2
                    more = not (last and k == UNROLL - 1)
                    next_pair = k % 2 == 1 and not (last and j == 1)
                    pair_after = k % 2 == 0 and not last
                    scores(st, k, 0)
                    if full and more:
                        score_maxes(st, k + 1, 0)
                    scores(st, k, 1)
                    if full and more:
                        score_maxes(st, k + 1, 1)
                    add_outputs(st, k, 0)
                    scores(st, k, 2)
                    if full and more:
                        score_maxes(st, k + 1, 2)
                    add_outputs(st, k, 1)
                    if full and next_pair:
                        wait(pe, s_qk, st.pair(j + (1 if last else 2)) + (1 - NPAIR))
                        v_products(st, j + 1)
                    scores(st, k, 3)
                    if full and more:
                        score_maxes(st, k + 1, 3)
                    add_outputs(st, k, 2)
                    if pair_after:
                        if full:
                            wait(pe, s_v, st.batch(2 * (j + 1)))
                        transposes(st, j + 2)
                    add_outputs(st, k, 3)
                    if full and more:
                        max_transposed(st, k + 1)
                    out_transposed(st, k)
                    if full:
                        if layer == FFN:
                            attention_transposed(st, k)
                        if pair_after:
                            qk_products(st, j + 2)
                        out_projected(st, k)

                steps(pe, layer, slot)

            pe.wait_ge(s_v, 3 * B)
            pe.wait_ge(s_res, 3 * B + RES_CREDIT)
            with pe.Fori(0, NPAIR) as t:
                pe.wait_ge(s_xn, t * 2 + (3 * B + 2))
                for s in range(2):
                    last = tr(pb[:, s * S:(s + 1) * S], xn[:, 0, s, :])
                last.then_inc(s_t, 1)
                pe.wait_ge(s_hn2, t + 1)
            for n in range(B):
                last = mm(fb[:, n * E:(n + 1) * E], hn2T[:, n * S:(n + 1) * S], gate_w[:])
            last.then_inc(s_g, 1)

            pe.wait_ge(s_moe, 64)
            with pe.Fori(0, B) as n:
                hn = hn2T[:, bass.ds(n * S, S)]

                def hidden(e):
                    for c in range(FC):
                        last = mm(sbk[e % 2][:, c * S:(c + 1) * S], w1[:, e, c * 128:(c + 1) * 128], hn)
                    last.then_inc(s_up, 1)

                hidden(0)
                for e in range(E):
                    if e + 1 < E:
                        hidden(e + 1)
                    pe.wait_ge(s_mid2, n * E + (e + 1))
                    pe.wait_ge(s_acc, n * E + (e + 1 - 2 + ACC_CREDIT))
                    for c in range(FC):
                        mm(obk[e % 2][:, 0:D], mid[:, e % 2, c, :], w2[:, e, c, :], start=c == 0, stop=False)
                    mm(obk[e % 2][:, 0:D], ones_row[:], b2[:, e, :], start=False).then_inc(s_dn, 1)

        @block.scalar
        def _(act):
            def take_hT(st, j):
                i = j % 2
                wait(act, s_t, st.pair(j) + 1)
                wait(act, s_vp, st.pair(j) - NPAIR - 1)
                if st.layer == CROSS:
                    nc.scalar.copy(hT[:, i, :, :].rearrange("p a k -> p (a k)"), pb[:]).then_inc(s_hT, 1)
                else:
                    nc.scalar.activation(hT[:, i, 0, :], pb[:, 0:PAIR], ACT.Identity,
                                         bias=cols[:, 5:6], scale=cols[:, 4:5]).then_inc(s_hT, 1)

            def take_qk(st, j):
                wait(act, s_qkp, st.pair(j) + 1 - NPAIR)
                wait(act, s_r1, st.pair(j))
                if st.layer == CROSS:
                    nc.scalar.activation(qk[:, 0, :], pb[:, 0:PAIR], ACT.Identity, bias=xbq_scaled[:], scale=SCALE)
                    nc.scalar.activation(qk[:, 1, :], pb[:, PAIR:2 * PAIR], ACT.Identity,
                                         bias=cols[:, 1:2], scale=1.0).then_inc(s_qk, 1)
                else:
                    nc.scalar.activation(qk[:, 0, :], pb[:, 0:PAIR], ACT.Identity, bias=cols[:, 2:3], scale=1.0)
                    nc.scalar.activation(qk[:, 1, :], pb[:, PAIR:2 * PAIR], ACT.Identity,
                                         bias=cols[:, 3:4], scale=1.0).then_inc(s_qk, 1)

            def high_parts(st, j, writes):
                i = j % 2
                wait(act, s_wr[i], writes)
                if st.layer == SELF:
                    wait(act, s_t, st.pair(j) + 1)
                    nc.scalar.copy(parts[:, i, 0, 0, :], pb[:, 0:PAIR]).then_inc(s_hi, 1)
                else:
                    wait(act, s_qk, st.pair(j) + 1 - NPAIR)
                    nc.scalar.copy(parts[:, i, 0, :, :], qk[:]).then_inc(s_hi, 1)

            def middle_parts(st, j):
                i, n = j % 2, 1 if st.layer == SELF else 2
                wait(act, s_r1, st.pair(j) + 1)
                nc.scalar.copy(parts[:, i, 1, 0:n, :], rest[:, 0:n, :]).then_inc(s_mid, 1)

            def exponentials(st, k, g):
                wait(act, s_e, st.group(k, g) + 1)
                wait(act, s_pv, st.group(k, g) + (1 - 4 + PV_CREDIT))
                nc.scalar.activation(probs[:, g, :], sbk[g % 2][:], ACT.Exp,
                                     scale=1.0 if st.layer == CROSS else SCALE).then_inc(s_p, 1)

            def take_out(st, k):
                wait(act, s_pv, st.group(k, NG) + PV_CREDIT)
                wait(act, s_otr, st.batch(k) + (1 - 2 + OTR_CREDIT))
                nc.scalar.copy(outT[:, k % 2, :], obk[k % 2][:]).then_inc(s_oevac, 1)

            def take_attT(st, k):
                wait(act, s_atr, st.batch(k) + (1 - 2 * B))
                nc.scalar.copy(attT[:], fb[:, 0:S]).then_inc(s_attT, 1)

            act.sem_inc(s_p, P_CREDIT)
            act.sem_inc(s_oevac, OEV_CREDIT)
            act.wait_ge(s_dve_const, 5)
            for layer in (SELF, CROSS, FFN):
                z = Step(act, layer, 0)
                full = layer != SELF
                for j in range(2):
                    if full:
                        take_hT(z, j)
                        take_qk(z, j)
                    high_parts(z, j, z.turn(j) * WRITES)
                    middle_parts(z, j)

                def slot(st, k, last):
                    j = k // 2
                    pair_after = k % 2 == 0 and not last
                    exponentials(st, k, 0)
                    exponentials(st, k, 1)
                    if k % 2 == 1 and not last:
                        middle_parts(st, j + 2)
                    exponentials(st, k, 2)
                    exponentials(st, k, 3)
                    if pair_after and full:
                        take_hT(st, j + 2)
                    if pair_after and not full:
                        high_parts(st, j + 2, st.turn(j + 2) * WRITES)
                    take_out(st, k)
                    if layer == FFN:
                        take_attT(st, k)
                    if full:
                        if pair_after:
                            take_qk(st, j + 2)
                            high_parts(st, j + 2, st.turn(j + 2) * WRITES)

                steps(act, layer, slot)

            with act.Fori(0, NPAIR) as t:
                act.wait_ge(s_t, t + (3 * NPAIR + 1))
                nc.scalar.activation(hn2T[:, bass.ds(t * PAIR, PAIR)], pb[:, 0:PAIR], ACT.Identity,
                                     bias=cols[:, 7:8], scale=cols[:, 6:7]).then_inc(s_hn2, 1)
            with act.Fori(0, B) as n:
                for e in range(E):
                    act.wait_ge(s_up, n * E + (e + 1))
                    act.wait_ge(s_dn, n * E + (e + 1 - 2 + DN_CREDIT))
                    for c in range(FC):
                        last = nc.scalar.activation(mid[:, e % 2, c, :], sbk[e % 2][:, c * S:(c + 1) * S], ACT.Relu,
                                                    bias=b1[:, e, c:c + 1], scale=1.0)
                    last.then_inc(s_mid2, 1)

        @block.vector
        def _(dve):
            nc.vector.memset(stack[64:KROWS, :, :, :, :], 0.0).then_inc(s_dve_const, 1)
            nc.vector.memset(vaug[:], 0.0).then_inc(s_chain, 1)
            dve.wait_ge(s_chain, 1)
            nc.vector.memset(vaug[:, :, :, HD:HD + 1], 1.0).then_inc(s_dve_const, 1)
            nc.vector.memset(maxparts[:], 0.0).then_inc(s_dve_const, 1)
            nc.vector.memset(ones_row[:], 1.0).then_inc(s_chain, 1)
            dve.wait_ge(s_pool_const, 6)
            nc.vector.tensor_copy(identb[:], ident[:]).then_inc(s_dve_const, 1)
            dve.wait_ge(s_w, 16 * 15)
            nc.vector.tensor_scalar(xbq_scaled[:], cols[:, 0:1], SCALE, None, ALU.mult).then_inc(s_dve_const, 1)
            dve.sem_inc(s_res, RES_CREDIT)
            dve.sem_inc(s_mfree, MFREE_CREDIT)
            dve.sem_inc(s_acc, ACC_CREDIT)
            dve.wait_ge(s_x, 32)

            def norm_no(st, j):
                return st.pair(j) if st.layer < FFN else (st.t * 4 + (2 * NPAIR + 2 * j))

            def row_stats(src, no):
                wait(dve, s_rstd, no, s_apart_dve)
                for s in range(2):
                    last = nc.vector.bn_stats(stats[:, s, :], src(s))
                last.then_inc(s_stats, 1)
                wait(dve, s_stats, no + 1, s_apart_dve)
                for s in range(2):
                    nc.vector.bn_aggr(meanvar[:, s, :], stats[:, s, :]).then_inc(s_mv, 1)

            def normalise(dst, src, no, sem_done):
                wait(dve, s_mv, no * 2 + 2)
                wait(dve, s_rstd, no + 1)
                for s in range(2):
                    nc.vector.tensor_scalar(dst(s), src(s), meanvar[:, s, 0:1], rstd[:, s:s + 1],
                                            ALU.subtract, ALU.mult).then_inc(sem_done, 1)

            def x_rows(st, j):
                return lambda s: x_sb[:, st.first + (2 * j + s), :]

            def y_rows(st, j):
                return lambda s: y_sb[:, st.first + (2 * j + s), :]

            def xn_rows(j):
                return lambda s: xn[:, j % 2, s, :]

            def norm_stats(st, j):
                row_stats(x_rows(st, j), norm_no(st, j))

            def norm_between(st, j):
                if st.layer == FFN:
                    no = norm_no(st, j)
                    normalise(y_rows(st, j), x_rows(st, j), no, s_y)
                    wait(dve, s_y, st.first + (2 * j + 2))
                    row_stats(y_rows(st, j), no + 1)

            def norm_rows(st, j):
                no = norm_no(st, j) + (1 if st.layer == FFN else 0)
                src = y_rows(st, j) if st.layer == FFN else x_rows(st, j)
                wait(dve, s_t, st.pair(j) - 1)
                if st.layer == SELF:
                    wait(dve, s_v, (st.pair(j) - 1) * 2)
                normalise(xn_rows(j), src, no, s_xn)

            def first_rest(st, j):
                i = j % 2
                wait(dve, s_hi, st.pair(j) + 1)
                wait(dve, s_lo, st.pair(j))
                if st.layer == SELF:
                    nc.vector.tensor_tensor(rest[:, 0, :], pb[:, 0:PAIR], parts[:, i, 0, 0, :],
                                            ALU.subtract).then_inc(s_r1, 1)
                else:
                    nc.vector.tensor_tensor(rest[:], qk[:], parts[:, i, 0, :, :], ALU.subtract).then_inc(s_r1, 1)

            def take_values(st, j):
                wait(dve, s_vp, st.pair(j) + 1 - NPAIR)
                wait(dve, s_pv, (st.pair(j) * 2 - 2) * NG + PV_CREDIT)
                row = rows[:, 0 if st.layer == CROSS else 2, :]
                for s in range(2):
                    nc.vector.tensor_tensor(vaug[:, (2 * j + s) % UNROLL, :, 0:HD],
                                            pb[:, s * S:(s + 1) * S].rearrange("p (h d) -> p h d", d=HD),
                                            row.rearrange("p (h d) -> p h d", d=HD), ALU.add).then_inc(s_v, 1)

            def row_maxes(st, k, g):
                bank = mbk[(k * PERM_M + g) % 2]
                if st.layer == CROSS and g == 0:
                    wait(dve, s_bias[k % 4], (st.t + k // 4) * (16 * NG) + 16 * NG)
                wait(dve, s_mp, st.maxuse(k, g) + 1, s_apart_dve)
                if st.layer == CROSS:
                    for h in range(G):
                        head = g * G + h
                        last = nc.vector.tensor_tensor_reduce(
                            out=bank[:, h * S:(h + 1) * S], in0=bank[:, h * S:(h + 1) * S], in1=bias_in[:, k % 4, head, :], scale=1.0,
                            scalar=-3.0e38, op0=ALU.add, op1=ALU.max, accum_out=rowmax[:, head:head + 1])
                else:
                    last = nc.vector.tensor_reduce(rowmax[:, g * G:(g + 1) * G],
                                                   bank[:].rearrange("p (h k) -> p h k", h=G), AX.X, ALU.max)
                last.then_inc(s_mfree, 1)

            def max_parts(st, k):
                wait(dve, s_mfree, st.maxuse(k, NG) + MFREE_CREDIT)
                nc.vector.tensor_scalar(maxparts[:, 0:NH], rowmax[:], -1.0, None, ALU.mult).then_inc(s_mhi, 1)
                wait(dve, s_mhi, st.batch(k) + (1 - B))
                nc.vector.scalar_tensor_tensor(out=maxparts[:, NH:2 * NH], in0=rowmax[:], scalar=-1.0,
                                               in1=maxparts[:, 0:NH], op0=ALU.mult,
                                               op1=ALU.subtract).then_inc(s_mparts, 1)

            def take_maxT(st, k):
                wait(dve, s_mp, st.maxuse(k, NG) + 1)
                wait(dve, s_e, (st.batch(k) - 1) * NG)
                nc.vector.tensor_copy(maxT[:, k % 2, :],
                                      mbk[(k * PERM_M + NG) % 2][:].bitcast(bf16)[:, 0:128]).then_inc(s_mfree, 1)

            def attention(st, k):
                wait(dve, s_otr, st.batch(k) + (1 + OTR_CREDIT))
                o = fb[:].rearrange("p (h c) -> p h c", c=VC)
                nc.vector.reciprocal(rowsum_inv[:], o[:, :, HD]).then_inc(s_inv, 1)
                wait(dve, s_inv, st.batch(k) + 1)
                if st.layer == CROSS:
                    nc.vector.tensor_tensor(inv_sel[:], rowsum_inv[:].unsqueeze(2).to_broadcast([128, NH, TQ]),
                                            in_block[:].unsqueeze(1).to_broadcast([128, NH, TQ]),
                                            ALU.mult).then_inc(s_invsel, 1)
                    wait(dve, s_invsel, st.batch(k) + (1 - B))
                    nc.vector.tensor_tensor(
                        att_sel[:], o[:, :, 0:HD].rearrange("p h d -> p d h").unsqueeze(3).to_broadcast([128, HD, NH, TQ]),
                        inv_sel[:].unsqueeze(1).to_broadcast([128, HD, NH, TQ]), ALU.mult).then_inc(s_att, 1)
                    return
                nc.vector.tensor_tensor(att[:].rearrange("p (h d) -> p h d", d=HD), o[:, :, 0:HD],
                                        rowsum_inv[:].unsqueeze(2).to_broadcast([128, NH, HD]),
                                        ALU.mult).then_inc(s_att, 1)
                if st.layer == SELF:
                    wait(dve, s_att, st.batch(k) + 1)
                    r = x_sb[:, st.first + k, :]
                    nc.vector.tensor_tensor(r, r, att[:], ALU.add).then_inc(s_res, 1)

            def residual(st, k):
                res = x_sb if st.layer == CROSS else y_sb
                if k % 2 == 0:
                    wait(dve, s_resbias, st.pair(k // 2) + (1 - NPAIR))
                wait(dve, s_oproj, st.batch(k) + (1 - B))
                r = res[:, st.first + k, :]
                nc.vector.tensor_tensor(r, fb[:, 0:D], r, ALU.add).then_inc(s_res, 1)

            for layer in (SELF, CROSS, FFN):
                z = Step(dve, layer, 0)
                full = layer != SELF
                if layer != SELF:
                    wait(dve, s_res, B * layer + RES_CREDIT)
                for j in range(2):
                    norm_stats(z, j)
                    norm_between(z, j)
                    norm_rows(z, j)
                    first_rest(z, j)
                    if full and j == 0:
                        take_values(z, 0)
                if full:
                    for g in range(NG):
                        row_maxes(z, 0, g)
                    max_parts(z, 0)
                    take_maxT(z, 0)

                def slot(st, k, last):
                    j = k // 2
                    more = not (last and k == UNROLL - 1)
                    next_pair = k % 2 == 1 and not (last and j == 1)
                    pair_after = k % 2 == 0 and not last
                    rest_due = k % 2 == 1 and not last
                    if full and more:
                        row_maxes(st, k + 1, 0)
                    if rest_due:
                        first_rest(st, j + 2)
                    if pair_after:
                        norm_stats(st, j + 2)
                    if full and more:
                        row_maxes(st, k + 1, 1)
                    if pair_after:
                        norm_between(st, j + 2)
                    if full and more:
                        row_maxes(st, k + 1, 2)
                    if full and next_pair:
                        take_values(st, j + 1)
                    if pair_after:
                        norm_rows(st, j + 2)
                    if full and more:
                        row_maxes(st, k + 1, 3)
                        max_parts(st, k + 1)
                        take_maxT(st, k + 1)
                    attention(st, k)
                    if full:
                        residual(st, k)

                steps(dve, layer, slot)

            dve.wait_ge(s_res, 3 * B + RES_CREDIT)
            with dve.Fori(0, NPAIR) as t:
                rows_of = lambda s: y_sb[:, t * 2 + s, :]
                row_stats(rows_of, t + 4 * NPAIR)
                dve.wait_ge(s_t, t + 3 * NPAIR)
                normalise(lambda s: xn[:, 0, s, :], rows_of, t + 4 * NPAIR, s_xn)

            chain = [2]

            def link(ins):
                chain[0] += 1
                ins.then_inc(s_chain, 1)
                dve.wait_ge(s_chain, chain[0])

            dve.wait_ge(s_g, 1)
            over_b = lambda t: t[:].unsqueeze(1).to_broadcast([128, B, E])
            over_e = lambda t: t[:].unsqueeze(2).to_broadcast([128, B, E])
            link(nc.vector.tensor_tensor(logits[:], fb[:, 0:B * E].rearrange("p (b e) -> p b e", e=E),
                                         over_b(gate_b), ALU.add))
            link(nc.vector.tensor_reduce(best[:], logits[:], AX.X, ALU.max))
            link(nc.vector.tensor_tensor(is_best[:], logits[:], over_e(best), ALU.is_equal))
            link(nc.vector.tensor_scalar(is_best[:], is_best[:], -float(E), float(E), ALU.mult, ALU.add))
            link(nc.vector.tensor_tensor(place[:], is_best[:], over_b(expert_no), ALU.add))
            link(nc.vector.tensor_reduce(first_best[:], place[:], AX.X, ALU.min))
            link(nc.vector.tensor_tensor(onehot[:], over_b(expert_no), over_e(first_best), ALU.is_equal))

            dve.wait_ge(s_rr, NPAIR)
            with dve.Fori(0, B) as n:
                r = x_sb[:, n, :]
                for e in range(E):
                    dve.wait_ge(s_dn, n * E + (e + 1 + DN_CREDIT))
                    dve.wait_ge(s_acc, n * E + (e + ACC_CREDIT))
                    nc.vector.scalar_tensor_tensor(out=r, in0=obk[e % 2][:, 0:D], scalar=onehot[:, n, e:e + 1],
                                                   in1=r, op0=ALU.mult, op1=ALU.add).then_inc(s_acc, 1)


def kernel(**inputs):
    import concourse.bacc as bacc
    from concourse.bass_utils import run_bass_kernel_spmd

    g = {k: np.ascontiguousarray(v) for k, v in inputs.items()}
    x_ = lambda n: g["L0_xattn_" + n]
    f_ = lambda n: g["L0_ffn_" + n]
    arrays = {
        "x": g["x"], "ctx": g["ctx_1024"], "bias": g["fside_Bx16xSxS2_0"],
        "w_xq": x_("Wq").T, "w_xk": x_("Wk").T, "w_xv": x_("Wv").T, "w_xo": x_("Wo").T,
        "w_fq": f_("wq"), "w_fk": f_("wk"), "w_fv": f_("wv"), "w_fo": f_("wo"),
        "cols": np.stack([x_("bq"), x_("bk"), f_("bq"), f_("bk"), f_("ln1_g"), f_("ln1_b"),
                          f_("ln2_g"), f_("ln2_b")], axis=1),
        "xbv": x_("bv"), "xbo": x_("bo"), "fbv": f_("bv"), "fbo": f_("bo"),
        "gate_w": f_("gate_w"), "gate_b": f_("gate_b"), "w1": f_("w1"), "w2": f_("w2"),
        "b1": f_("b1").reshape(E, FC, 128).transpose(2, 0, 1), "b2": f_("b2").reshape(1, E, D),
    }
    arrays = {k: np.ascontiguousarray(v) for k, v in arrays.items()}
    nc = bacc.Bacc("TRN2", target_bir_lowering=False, num_devices=1)
    aps = {k: nc.dram_tensor("in_" + k, v.shape, mybir.dt.from_np(v.dtype), kind="ExternalInput").ap()
           for k, v in arrays.items()}
    out = nc.dram_tensor("out", (B, S, D), mybir.dt.float32, kind="ExternalOutput").ap()
    build(nc, aps, out)
    r = run_bass_kernel_spmd(nc, [{"in_" + k: v for k, v in arrays.items()}], core_ids=[0])
    return r.results[0]["out"]
```

```python
import numpy as np
from contextlib import ExitStack

import concourse.bass as bass
from concourse import mybir

B, S, D = 16, 128, 128
NH, HD = 16, 8
E, F = 8, 512
FC = F // 128
EPS = 1e-5
SCALE = HD ** -0.5
G = 4
NG = NH // G
PAIR = 2 * S
NPAIR = B // 2
UNROLL = 4
NT = 3
ROWS = NT * NT * HD
KROWS = 96
VC = 32
MASKED = -1e30
TR = D // HD
TQ = S // TR

TILE = 128
NTILES = B * S // TILE + E - 1
TBUF = 4
WIDTH = 2 * D + 1

SELF, CROSS, FFN = 0, 1, 2
PERM_M = NG + 1


def wait(eng, sem, value, apart=None):
    if not isinstance(value, int) or value > 0:
        eng.wait_ge(sem, value)
        if apart is not None and not isinstance(value, int):
            eng.sem_inc(apart, 1)


class Step:

    def __init__(self, eng, layer, t):
        fixed = isinstance(t, int)
        snap = (lambda v: v) if fixed else eng.snap
        self.layer, self.t = layer, t
        self.first = snap(t * UNROLL)
        self.groups = snap(t * (UNROLL * NG))
        self.maxes = snap(t * (UNROLL * PERM_M))

    def batch(self, k):
        return self.first + (B * self.layer + k)

    def group(self, k, g):
        return self.groups + (B * NG * self.layer + k * NG + g)

    def maxuse(self, k, g):
        return self.maxes + (B * PERM_M * (self.layer - 1) + k * PERM_M + g)

    def pair(self, j):
        return self.t * 2 + (NPAIR * self.layer + j)

    def turn(self, j):
        return self.t + (NPAIR // 2 * self.layer + j // 2)


def build(nc, a, out):
    f32, bf16, i32 = mybir.dt.float32, mybir.dt.bfloat16, mybir.dt.int32
    ALU, ACT, AX = mybir.AluOpType, mybir.ActivationFunctionType, mybir.AxisListType

    ctx = ExitStack()
    with ctx:
        def sb(name, shape, dt=f32):
            return ctx.enter_context(nc.sbuf_tensor(name, shape, dt))

        def sem(name):
            return ctx.enter_context(nc.semaphore(name))

        x_sb = sb("x_sb", [128, B, D])
        y_sb = sb("y_sb", [128, B, D])
        xn = sb("xn", [128, 2, 2, D])
        stats = sb("stats", [128, 2, 6])
        meanvar = sb("meanvar", [128, 2, 2])
        vareps = sb("vareps", [128, 2])
        rstd = sb("rstd", [128, 2])
        ctx_in = sb("ctx_in", [128, 2, 2, D])
        hT = sb("hT", [128, 2, 2, PAIR])
        qk = sb("qk", [128, 2, PAIR])
        rest = sb("rest", [128, 2, PAIR])
        parts = sb("parts", [128, 2, NT, 2, PAIR], bf16)
        stack = sb("stack", [KROWS, 2, 2, NH, PAIR], bf16)
        vaug = sb("vaug", [128, UNROLL, NH, VC])
        bias_in = sb("bias_in", [128, 4, NH, S])
        rows_out = bias_in[:].rearrange("p a h k -> p (a h k)")[:, 0:B * WIDTH].rearrange("p (b w) -> p b w", w=WIDTH)
        probs = sb("probs", [128, NG, G * S])
        rowmax = sb("rowmax", [128, NH])
        maxparts = sb("maxparts", [128, 128], bf16)
        maxT = sb("maxT", [128, 2, 128], bf16)
        outT = sb("outT", [128, 2, NG * S])
        rowsum_inv = sb("rowsum_inv", [128, NH])
        att = sb("att", [128, D])
        attT = sb("attT", [128, S])
        ident = sb("ident", [128, 128])
        identb = sb("identb", [128, 128], bf16)
        causal = sb("causal", [128, S], bf16)
        pick = sb("pick", [128, NH, S], bf16)
        minus_half = sb("minus_half", [128, 2])
        in_block = sb("in_block", [128, TQ])
        inv_sel = sb("inv_sel", [128, NH, TQ])
        att_sel = sb("att_sel", [128, HD, NH, TQ])
        wxo = sb("wxo", [128, HD, D])
        wx = {k: sb("w_" + k, [128, D]) for k in ("xq", "xk", "xv", "fq", "fk", "fv", "fo")}
        cols = sb("cols", [128, 8])
        xbq_scaled = sb("xbq_scaled", [128, 1])
        rows = sb("rows", [128, 4, D])
        gate_w = sb("gate_w", [128, E])
        gate_b = sb("gate_b", [128, E])
        w1 = sb("w1", [128, E, F])
        w2 = sb("w2", [128, E, FC, D])
        b1_rows = sb("b1_rows", [128, E, F])
        b2_rows = sb("b2_rows", [128, E, D])
        hn2T = sb("hn2T", [128, B * S])
        logits = sb("logits", [128, B, E])
        best = sb("best", [128, B])
        is_best = sb("is_best", [128, B, E])
        expert_no = sb("expert_no", [128, E])
        place = sb("place", [128, B, E])
        first_best = sb("first_best", [128, B])
        onehot = sb("onehot", [128, B, E])
        before = sb("before", [128, 128])
        ones = sb("ones", [128, 128])
        prefix = sb("prefix", [128, 2, B // 2 + B, E])
        tile_ends = sb("tile_ends", [128, B])
        over_end = sb("over_end", [128, E, B])
        starts = sb("starts", [128, 2, E // 2 + E])
        place_in = sb("place_in", [128, B, E])
        position = sb("position", [128, B])
        position_i = sb("position_i", [128, B], i32)
        tile_no = sb("tile_no", [128, NTILES])
        started = sb("started", [1, NTILES, E])
        tile_expert = sb("tile_expert", [1, NTILES])
        tile_expert_i = sb("tile_expert_i", [1, NTILES], i32)
        filler = sb("filler", [128, WIDTH])
        tile_xn = outT[:].rearrange("p b (t d) -> p (b t) d", d=D)[:, 0:TBUF, :]
        tile_res = vaug[:].rearrange("p b h c -> p (b h c)")[:, 0:TBUF * (WIDTH - D)].rearrange("p (b w) -> p b w", w=WIDTH - D)
        hn2T_tile, moe = xn[:, 0, :, :], xn[:, 1, :, :]
        mid, midT = probs[:, 0:2, :], probs[:, 2:4, :]

        pb = ctx.enter_context(nc.psum_tensor("prep_bank", [128, 512], f32))
        fb = ctx.enter_context(nc.psum_tensor("finish_bank", [128, 512], f32))
        sbk = [ctx.enter_context(nc.psum_tensor(f"score_bank{i}", [128, G * S], f32)) for i in range(2)]
        mbk = [ctx.enter_context(nc.psum_tensor(f"max_bank{i}", [128, G * S], f32)) for i in range(2)]
        obk = [ctx.enter_context(nc.psum_tensor(f"out_bank{i}", [128, NG * S], f32)) for i in range(2)]

        scratch = nc.dram_tensor("parts_scratch", (2, 2, NT, HD, NH, PAIR), bf16, kind="Internal").ap()
        row_elems = NH * PAIR
        routed = nc.dram_tensor("routed_rows", (NTILES * TILE, WIDTH), f32, kind="Internal").ap()

        WRITES, READS = 2 * 16, (NT + 1) * 16

        s_apart_dve = sem("waited_apart_dve")
        s_apart_pool = sem("waited_apart_pool")
        s_x = sem("x_loaded")
        s_w = sem("weights_loaded")
        s_moe = sem("expert_weights_loaded")
        s_ctx = [sem(f"ctx_loaded{i}") for i in range(2)]
        s_bias = [sem(f"bias_loaded{i}") for i in range(4)]
        s_wr = [sem(f"scratch_written{i}") for i in range(2)]
        s_stack = [sem(f"stack_loaded{i}") for i in range(2)]
        s_out = sem("out_stored")
        s_pool_const = sem("pool_constants")
        s_dve_const = sem("dve_constants")
        s_stats = sem("stats_ready")
        s_mv = sem("meanvar_ready")
        s_ve = sem("vareps_ready")
        s_rstd = sem("rstd_ready")
        s_y = sem("ffn_input_ready")
        s_xn = sem("xn_ready")
        s_t = sem("transposed")
        s_hT = sem("hT_ready")
        s_qkp = sem("qk_products")
        s_qk = sem("qk_ready")
        s_hi = sem("high_parts")
        s_r1 = sem("first_rest")
        s_mid = sem("middle_parts")
        s_lo = sem("low_parts")
        s_resbias = sem("residual_biased")
        s_vp = sem("v_products")
        s_v = sem("v_ready")
        s_mp = sem("max_products")
        s_mfree = sem("max_bank_free")
        s_mhi = sem("max_high_part")
        s_mparts = sem("max_parts")
        s_e = sem("scores_ready")
        s_p = sem("probs_ready")
        s_pv = sem("outputs_added")
        s_oevac = sem("out_copied")
        s_otr = sem("out_transposed")
        s_inv = sem("rowsum_inverted")
        s_invsel = sem("inverse_in_block")
        s_att = sem("attention_ready")
        s_atr = sem("attention_transposed")
        s_attT = sem("attT_ready")
        s_oproj = sem("out_projected")
        s_res = sem("residual_done")
        s_g = sem("gate_products")
        s_hn2 = sem("hn2T_ready")
        s_copied = sem("rows_copied")
        s_rr = sem("rows_summed")
        s_chain = sem("gate_chain")
        s_onehot = sem("choices_ready")
        s_rank = sem("rank_products")
        s_route = sem("positions_ready")
        s_fill = sem("filler_written")
        s_routed = sem("rows_routed")
        s_values = [sem(f"values_loaded{i}") for i in range(TBUF)]
        s_residuals = [sem(f"residuals_loaded{i}") for i in range(TBUF)]
        s_stored = [sem(f"tile_stored{i}") for i in range(TBUF)]
        s_xT = sem("tile_transposed")
        s_tT = sem("hn2T_tile_ready")
        s_up = sem("hidden_products")
        s_mid2 = sem("hidden_biased")
        s_midp = sem("hidden_transposed")
        s_midT = sem("midT_ready")
        s_dn = sem("expert_output")
        s_moe_out = sem("moe_ready")
        s_sum = sem("tile_summed")

        P_CREDIT, PV_CREDIT, OEV_CREDIT, OTR_CREDIT, RES_CREDIT, MFREE_CREDIT = 2, 4, 2, 2, 1, 2
        SUM_CREDIT, COPY_CREDIT, HN2_CREDIT, MIDT_CREDIT, DN_CREDIT = 2, 2, 1, 1, 1

        block = ctx.enter_context(nc.Block())

        def steps(eng, layer, slot):
            def body(t, last):
                st = Step(eng, layer, t)
                for k in range(UNROLL):
                    slot(st, k, last)
            with eng.Fori(0, B // UNROLL - 1) as t:
                body(t, False)
            body(B // UNROLL - 1, True)

        def tile_slots(eng, slot):
            slot(0, 0)
            with eng.Fori(0, (NTILES - 3) // TBUF) as t:
                for k in range(1, TBUF + 1):
                    slot(eng.snap(t * TBUF + k), k)
            for s in range(NTILES - 2, NTILES + 1):
                slot(s, s)

        def due(s, k, ahead):
            return 0 <= s + ahead < NTILES if isinstance(s, int) else True

        @block.sync
        def _(sp):
            xr = a["x"].rearrange("b s d -> s b d")
            sp.dma_start(x_sb[:, 0:4, :], xr[:, 0:4, :]).then_inc(s_x, 16)
            sp.dma_start(x_sb[:, 4:B, :], xr[:, 4:B, :]).then_inc(s_x, 16)
            for k in wx:
                sp.dma_start(wx[k][:], a["w_" + k]).then_inc(s_w, 16)
            sp.dma_start(wxo[:].rearrange("p d n -> p (d n)"),
                         bass.AP(tensor=a["w_xo"].tensor, offset=a["w_xo"].offset,
                                 ap=[[0, TQ], [HD * D, TR], [1, HD * D]])).then_inc(s_w, 16)
            sp.dma_start(cols[:], a["cols"]).then_inc(s_w, 16)
            for i, k in enumerate(("xbv", "xbo", "fbv", "fbo")):
                sp.dma_start(rows[:, i, :], a[k].partition_broadcast(128)).then_inc(s_w, 16)
            sp.dma_start(gate_w[:], a["gate_w"]).then_inc(s_w, 16)
            sp.dma_start(gate_b[:], a["gate_b"].partition_broadcast(128)).then_inc(s_w, 16)

            def write_parts(layer, turn, i, pair_no):
                wait(sp, s_lo, pair_no + 1)
                wait(sp, s_stack[i], turn * READS)
                for w in range(1 if layer == SELF else 2):
                    sp.dma_start(scratch[i, w].rearrange("p d h k -> (d h) p k"),
                                 parts[:, i, :, w, :]).then_inc(s_wr[i], 16)
                if layer == SELF:
                    sp.sem_inc(s_wr[i], WRITES // 2)

            def read_stack(layer, turn, i, pair_no):
                wait(sp, s_wr[i], turn * WRITES + WRITES)
                wait(sp, s_e, pair_no * (2 * NG) - 2 * (2 * NG) + 2 * NG)
                wk = 0 if layer == SELF else 1
                for part in range(NT):
                    q_src = bass.AP(tensor=scratch.tensor, offset=scratch[i, 0, part].offset,
                                    ap=[[0, NT], [row_elems, HD], [1, row_elems]])
                    r0 = part * NT * HD
                    sp.dma_start(stack[r0:r0 + NT * HD, i, 0, :, :], q_src).then_inc(s_stack[i], 16)
                k_src = bass.AP(tensor=scratch.tensor, offset=scratch[i, wk].offset,
                                ap=[[0, NT], [row_elems, NT * HD], [1, row_elems]])
                sp.dma_start(stack[0:ROWS, i, 1, :, :], k_src).then_inc(s_stack[i], 16)

            def load_bias(n, batch_no, i, turn):
                wait(sp, s_e, (batch_no - 3) * NG)
                src = a["bias"][bass.ds(n, 1)].rearrange("o h q k -> q (o h) k")
                for half in range(2):
                    heads = slice(half * NH // 2, (half + 1) * NH // 2)
                    sp.dma_start(bias_in[:, i, heads, :], src[:, heads, :]).then_inc(s_bias[i], 16)

            def load_ctx(first, i, pair_no):
                wait(sp, s_t, pair_no - 1)
                sp.dma_start(ctx_in[:, i, :, :],
                             a["ctx"][bass.ds(first, 2)].rearrange("b s d -> s b d")).then_inc(s_ctx[i], 16)

            sp.wait_ge(s_dve_const, 1)
            for layer in (SELF, CROSS, FFN):
                z = Step(sp, layer, 0)
                if layer == CROSS:
                    for n in range(3):
                        load_bias(n, z.batch(n), n, 0)
                    for j in range(2):
                        load_ctx(2 * j, j, z.pair(j))
                if layer == SELF:
                    sp.dma_start(w1[:], a["w1"].rearrange("e h f -> h e f")).then_inc(s_moe, 16)
                    sp.dma_start(w2[:], a["w2"].rearrange("e (c p) h -> p e c h", p=128)).then_inc(s_moe, 16)
                    sp.dma_start(b1_rows[:], a["b1"].partition_broadcast(128)).then_inc(s_moe, 16)
                    sp.dma_start(b2_rows[:], a["b2"].partition_broadcast(128)).then_inc(s_moe, 16)
                    sp.wait_ge(s_pool_const, 18)
                    sp.dma_start(routed.rearrange("(t p) w -> p t w", p=TILE),
                                 filler[:].unsqueeze(1).to_broadcast([128, NTILES, WIDTH])).then_inc(s_fill, 16)
                write_parts(layer, z.turn(0), 0, z.pair(0))
                read_stack(layer, z.turn(0), 0, z.pair(0))
                write_parts(layer, z.turn(1), 1, z.pair(1))

                def slot(st, k, last):
                    j = k // 2
                    if layer == CROSS and k % 2 == 0 and not last:
                        load_ctx(st.first + 2 * (j + 2), j, st.pair(j + 2))
                    if k % 2 == 0 and not (last and j == 1):
                        read_stack(layer, st.turn(j + 1), (j + 1) % 2, st.pair(j + 1))
                    if layer == CROSS and not (last and k >= 1):
                        load_bias(st.first + (k + 3), st.batch(k + 3), (k + 3) % 4, 0)
                    if k % 2 == 1 and not last:
                        write_parts(layer, st.turn(j + 2), j, st.pair(j + 2))

                steps(sp, layer, slot)

            sp.wait_ge(s_routed, 16 * B)

            def load_values(i, buf):
                wait(sp, s_xT, i + (1 - TBUF))
                sp.dma_start(tile_xn[:, buf, :], routed[bass.ds(i * TILE, TILE), 0:D]).then_inc(s_values[buf], 16)

            def load_residuals(i, buf):
                wait(sp, s_stored[buf], (i - buf) * (16 // TBUF))
                sp.dma_start(tile_res[:, buf, :], routed[bass.ds(i * TILE, TILE), D:WIDTH]).then_inc(s_residuals[buf], 16)

            for i in range(TBUF):
                load_values(i, i)
            for i in range(TBUF - 2):
                load_residuals(i, i)
            with sp.Fori(0, NTILES // TBUF - 1) as t:
                for k in range(TBUF):
                    i = sp.snap(t * TBUF + (TBUF + k))
                    load_values(i, k)
                    load_residuals(i - 2, (k - 2) % TBUF)
            for i in range(NTILES // TBUF * TBUF, NTILES + 2):
                if i < NTILES:
                    load_values(i, i % TBUF)
                load_residuals(i - 2, (i - 2) % TBUF)
            for i in range(TBUF):
                sp.wait_ge(s_stored[i], 16 * ((NTILES - 1 - i) // TBUF + 1))

        @block.gpsimd
        def _(pool):
            nc.gpsimd.memset(ident[:], 0.0).then_inc(s_pool_const, 1)
            nc.gpsimd.memset(minus_half[:], -0.5).then_inc(s_pool_const, 1)
            nc.gpsimd.memset(causal[:], 0.0).then_inc(s_pool_const, 1)
            nc.gpsimd.memset(pick[:], 0.0).then_inc(s_pool_const, 1)
            nc.gpsimd.memset(in_block[:], 1.0).then_inc(s_pool_const, 1)
            pool.wait_ge(s_pool_const, 5)
            nc.gpsimd.affine_select(out=ident[:], in_=ident[:], compare_op=ALU.not_equal, fill=1.0, base=0,
                                    pattern=[[-1, 128]], channel_multiplier=1).then_inc(s_pool_const, 1)
            nc.gpsimd.affine_select(out=causal[:], in_=causal[:], compare_op=ALU.is_ge, fill=MASKED, base=0,
                                    pattern=[[1, S]], channel_multiplier=-1).then_inc(s_pool_const, 1)
            nc.gpsimd.affine_select(out=pick[:], in_=pick[:], compare_op=ALU.not_equal, fill=1.0, base=0,
                                    pattern=[[-1, NH], [0, S]], channel_multiplier=1).then_inc(s_pool_const, 1)
            nc.gpsimd.affine_select(out=in_block[:], in_=in_block[:], compare_op=ALU.is_ge, fill=0.0, base=0,
                                    pattern=[[-TR, TQ]], channel_multiplier=1).then_inc(s_pool_const, 1)
            pool.wait_ge(s_pool_const, 9)
            nc.gpsimd.affine_select(out=in_block[:], in_=in_block[:], compare_op=ALU.is_ge, fill=0.0, base=TR - 1,
                                    pattern=[[TR, TQ]], channel_multiplier=-1).then_inc(s_pool_const, 1)
            nc.gpsimd.affine_select(out=pick[:], in_=pick[:], compare_op=ALU.not_equal, fill=1.0, base=-NH,
                                    pattern=[[-1, NH], [0, S]], channel_multiplier=1).then_inc(s_pool_const, 1)
            nc.gpsimd.iota(expert_no[:], pattern=[[1, E]], base=0, channel_multiplier=0,
                           allow_small_or_imprecise_dtypes=True).then_inc(s_pool_const, 1)
            nc.gpsimd.memset(before[:], 1.0).then_inc(s_pool_const, 1)
            nc.gpsimd.memset(filler[:], 0.0).then_inc(s_pool_const, 1)
            nc.gpsimd.iota(tile_ends[:], pattern=[[TILE, B]], base=0, channel_multiplier=0,
                           allow_small_or_imprecise_dtypes=True).then_inc(s_pool_const, 1)
            nc.gpsimd.iota(tile_no[:], pattern=[[1, NTILES]], base=0, channel_multiplier=0,
                           allow_small_or_imprecise_dtypes=True).then_inc(s_pool_const, 1)
            pool.wait_ge(s_pool_const, 16)
            nc.gpsimd.affine_select(out=before[:], in_=before[:], compare_op=ALU.is_gt, fill=0.0, base=0,
                                    pattern=[[1, 128]], channel_multiplier=-1).then_inc(s_pool_const, 1)
            nc.gpsimd.iota(filler[:].bitcast(i32)[:, 2 * D:WIDTH], pattern=[[0, 1]], base=B * S,
                           channel_multiplier=1).then_inc(s_pool_const, 1)
            pool.wait_ge(s_w, 16 * 15)

            def inverse_deviation(norm_no):
                wait(pool, s_mv, norm_no * 2 + 2, s_apart_pool)
                nc.gpsimd.tensor_scalar(vareps[:], meanvar[:, :, 1], EPS, None, ALU.add).then_inc(s_ve, 1)
                wait(pool, s_ve, norm_no + 1)
                nc.gpsimd.tensor_tensor(rstd[:], vareps[:], minus_half[:], ALU.pow).then_inc(s_rstd, 1)

            def norm_no(st, j):
                return st.pair(j) if st.layer < FFN else (st.t * 4 + (2 * NPAIR + 2 * j))

            def start_pair(st, j):
                inverse_deviation(norm_no(st, j))
                if st.layer == FFN:
                    inverse_deviation(norm_no(st, j) + 1)
                if st.layer != SELF:
                    wait(pool, s_xn, st.pair(j) * 2 + 2)
                    res = x_sb if st.layer == CROSS else y_sb
                    row = rows[:, 1 if st.layer == CROSS else 3, :]
                    for s in range(2):
                        r = res[:, st.first + (2 * j + s), :]
                        last = nc.gpsimd.tensor_tensor(r, r, row, ALU.add)
                    last.then_inc(s_resbias, 1)

            def low_parts(st, j):
                i = j % 2
                n = 1 if st.layer == SELF else 2
                wait(pool, s_mid, st.pair(j) + 1)
                nc.gpsimd.tensor_tensor(parts[:, i, 2, 0:n, :], rest[:, 0:n, :], parts[:, i, 1, 0:n, :],
                                        ALU.subtract).then_inc(s_lo, 1)

            def self_values(st, j):
                wait(pool, s_xn, st.pair(j) * 2 + 2)
                for s in range(2):
                    wait(pool, s_pv, (st.pair(j) * 2 - 2) * NG + PV_CREDIT, s_apart_pool)
                    nc.gpsimd.tensor_copy(vaug[:, (2 * j + s) % UNROLL, :, 0:HD],
                                          xn[:, j % 2, s, :].rearrange("p (d h) -> p h d", d=HD)).then_inc(s_v, 1)

            pool.wait_ge(s_dve_const, 2)
            for layer in (SELF, CROSS, FFN):
                z = Step(pool, layer, 0)
                start_pair(z, 0)
                low_parts(z, 0)
                if layer == SELF:
                    self_values(z, 0)
                start_pair(z, 1)
                low_parts(z, 1)

                def slot(st, k, last):
                    j = k // 2
                    if k % 2 == 0 and not last:
                        start_pair(st, j + 2)
                    if k % 2 == 1:
                        if layer == SELF and not (last and j == 1):
                            self_values(st, j + 1)
                        if not last:
                            low_parts(st, j + 2)

                steps(pool, layer, slot)

            pool.wait_ge(s_e, 2 * B * NG)
            nc.gpsimd.iota(rows_out.bitcast(i32)[:, :, 2 * D], pattern=[[S, B]], base=0,
                           channel_multiplier=1).then_inc(s_rr, 1)
            with pool.Fori(0, NPAIR) as t:
                inverse_deviation(t + 4 * NPAIR)
                nc.gpsimd.tensor_tensor(rows_out[:, bass.ds(t * 2, 2), D:2 * D], x_sb[:, bass.ds(t * 2, 2), :],
                                        y_sb[:, bass.ds(t * 2, 2), :], ALU.add).then_inc(s_rr, 1)

            pool.wait_ge(s_fill, 16)
            pool.wait_ge(s_rr, NPAIR + 1)
            pool.wait_ge(s_copied, NPAIR + COPY_CREDIT)
            pool.wait_ge(s_route, 1)
            for n in range(B):
                nc.gpsimd.indirect_dma_start(
                    out=routed, out_offset=bass.IndirectOffsetOnAxis(ap=position_i[:, n:n + 1], axis=0),
                    in_=rows_out[:, n, :], in_offset=None).then_inc(s_routed, 16)

            def store_tile(i, buf):
                wait(pool, s_sum, i + (1 + SUM_CREDIT), s_apart_pool)
                nc.gpsimd.indirect_dma_start(
                    out=out.rearrange("b s d -> (b s) d"),
                    out_offset=bass.IndirectOffsetOnAxis(ap=tile_res[:, buf, :].bitcast(i32)[:, D:D + 1], axis=0),
                    in_=tile_res[:, buf, 0:D], in_offset=None,
                    bounds_check=B * S - 1, oob_is_err=False).then_inc(s_stored[buf], 16)

            with pool.Fori(0, NTILES // TBUF) as t:
                for k in range(TBUF):
                    store_tile(t * TBUF + k, k)
            for i in range(NTILES // TBUF * TBUF, NTILES):
                store_tile(i, i % TBUF)

        @block.tensor
        def _(pe):
            def mm(o, lhsT, rhs, start=True, stop=True, **kw):
                return nc.tensor.matmul(o, lhsT, rhs, start=start, stop=stop, **kw)

            def tr(o, src, stop=True):
                return nc.tensor.matmul(o, src, ident[:], start=True, stop=stop, is_transpose=True)

            def transposes(st, j):
                i = j % 2
                wait(pe, s_xn, st.pair(j) * 2 + 2)
                if st.layer == SELF:
                    wait(pe, s_r1, st.pair(j))
                elif st.layer == CROSS:
                    wait(pe, s_ctx[i], st.t * 16 + (j // 2 * 16 + 16))
                for s in range(2):
                    last = tr(pb[:, s * S:(s + 1) * S], xn[:, i, s, :])
                if st.layer == CROSS:
                    for s in range(2):
                        last = tr(pb[:, PAIR + s * S:PAIR + (s + 1) * S], ctx_in[:, i, s, :])
                last.then_inc(s_t, 1)

            def qk_products(st, j):
                i, key_side = j % 2, 1 if st.layer == CROSS else 0
                wq, wk = ("xq", "xk") if st.layer == CROSS else ("fq", "fk")
                wait(pe, s_hT, st.pair(j) + 1 - NPAIR)
                mm(pb[:, 0:PAIR], wx[wq][:], hT[:, i, 0, :])
                mm(pb[:, PAIR:2 * PAIR], wx[wk][:], hT[:, i, key_side, :]).then_inc(s_qkp, 1)

            def v_products(st, j):
                i, key_side = j % 2, 1 if st.layer == CROSS else 0
                wv = wx["xv" if st.layer == CROSS else "fv"]
                for s in range(2):
                    last = mm(pb[:, s * S:(s + 1) * S], hT[:, i, key_side, s * S:(s + 1) * S], wv[:])
                last.then_inc(s_vp, 1)

            def score_maxes(st, k, g):
                wait(pe, s_mfree, st.maxuse(k, g) + (1 - 2 + MFREE_CREDIT))
                if g == 0:
                    wait(pe, s_stack[k // 2 % 2], st.turn(k // 2) * READS + READS)
                i, s, bank = k // 2 % 2, k % 2, mbk[(k * PERM_M + g) % 2]
                for h in range(G):
                    last = mm(bank[:, h * S:(h + 1) * S],
                              stack[:, i, 0, g * G + h, s * S:(s + 1) * S], stack[:, i, 1, g * G + h, s * S:(s + 1) * S])
                last.then_inc(s_mp, 1)

            def max_transposed(st, k):
                wait(pe, s_mparts, st.batch(k) + (1 - B))
                wait(pe, s_mfree, st.maxuse(k, NG) + (1 - 2 + MFREE_CREDIT))
                bank = mbk[(k * PERM_M + NG) % 2]
                nc.tensor.transpose(bank[:].bitcast(bf16)[:, 0:128], maxparts[:], identb[:]).then_inc(s_mp, 1)

            def scores(st, k, g):
                i, s, bank = k // 2 % 2, k % 2, sbk[g % 2]
                wait(pe, s_p, st.group(k, g) + (1 - 2 + P_CREDIT))
                if g == 0:
                    wait(pe, s_stack[i], st.turn(k // 2) * READS + READS)
                    if st.layer == CROSS:
                        wait(pe, s_bias[k % 4], st.t * 32 + 32)
                    if st.layer != SELF:
                        wait(pe, s_mfree, st.maxuse(k, NG) + (1 + MFREE_CREDIT))
                for h in range(G):
                    o, head = bank[:, h * S:(h + 1) * S], g * G + h
                    q = stack[:, i, 0, head, s * S:(s + 1) * S]
                    key = stack[:, i, 1, head, s * S:(s + 1) * S]
                    if st.layer == SELF:
                        mm(o, identb[:], causal[:], stop=False)
                    elif st.layer == CROSS:
                        tr(o, bias_in[:, k % 4, head, :], stop=False)
                    last = mm(o, key, q, start=st.layer == FFN, stop=st.layer == SELF)
                    if st.layer != SELF:
                        last = mm(o, pick[:, head, :], maxT[:, k % 2, :], start=False)
                last.then_inc(s_e, 1)

            def add_outputs(st, k, g):
                wait(pe, s_p, st.group(k, g) + (1 + P_CREDIT))
                if g == 0:
                    wait(pe, s_v, st.batch(k) + (2 - k % 2))
                    wait(pe, s_oevac, st.batch(k) + (1 - 2 + OEV_CREDIT))
                for h in range(G):
                    last = mm(obk[k % 2][VC * h:VC * (h + 1), g * S:(g + 1) * S], vaug[:, k, g * G + h, :],
                              probs[:, g, h * S:(h + 1) * S], tile_position=(0, VC * h))
                last.then_inc(s_pv, 1)

            def out_transposed(st, k):
                wait(pe, s_oevac, st.batch(k) + (1 + OEV_CREDIT))
                wait(pe, s_res, st.batch(k) + (1 - 1 + RES_CREDIT))
                for g in range(NG):
                    last = tr(fb[:, g * S:(g + 1) * S], outT[:, k % 2, g * S:(g + 1) * S])
                last.then_inc(s_otr, 1)

            def attention_transposed(st, k):
                wait(pe, s_att, st.batch(k) + 1)
                tr(fb[:, 0:S], att[:]).then_inc(s_atr, 1)

            def out_projected(st, k):
                if st.layer == CROSS:
                    wait(pe, s_att, st.batch(k) + 1)
                    for d in range(HD):
                        last = mm(fb[:, 0:D], att_sel[:, d, :, :].rearrange("p h t -> p (h t)"), wxo[:, d, :],
                                  start=d == 0, stop=d == HD - 1)
                    last.then_inc(s_oproj, 1)
                else:
                    wait(pe, s_attT, st.batch(k) + (1 - 2 * B))
                    mm(fb[:, 0:D], attT[:], wx["fo"][:]).then_inc(s_oproj, 1)

            pe.sem_inc(s_pv, PV_CREDIT)
            pe.sem_inc(s_otr, OTR_CREDIT)
            pe.sem_inc(s_dn, DN_CREDIT)
            pe.wait_ge(s_pool_const, 12)
            pe.wait_ge(s_dve_const, 4)
            pe.wait_ge(s_w, 16 * 15)
            for layer in (SELF, CROSS, FFN):
                z = Step(pe, layer, 0)
                full = layer != SELF
                for j in range(2):
                    if layer == CROSS and j == 0:
                        pe.wait_ge(s_r1, NPAIR)
                    if layer == FFN and j == 0:
                        pe.wait_ge(s_v, 2 * B)
                    if full and j == 1:
                        wait(pe, s_v, z.batch(2))
                    transposes(z, j)
                    if full:
                        qk_products(z, j)
                        wait(pe, s_qk, z.pair(j) + 1 - NPAIR)
                    if full and j == 0:
                        v_products(z, 0)
                if full:
                    for g in range(NG):
                        score_maxes(z, 0, g)
                    max_transposed(z, 0)
                for g in range(NG // 2):
                    scores(z, 0, g)
                    if full:
                        score_maxes(z, 1, g)
                if full:
                    score_maxes(z, 1, 2)

                def slot(st, k, last):
                    j = k // 2
                    more = not (last and k >= UNROLL - 1)
                    more2 = not (last and k >= UNROLL - 2)
                    next_pair = k % 2 == 1 and not (last and j == 1)
                    pair_after = k % 2 == 0 and not last
                    add_outputs(st, k, 0)
                    if full and more:
                        score_maxes(st, k + 1, 3)
                    scores(st, k, 2)
                    add_outputs(st, k, 1)
                    scores(st, k, 3)
                    if full and more:
                        max_transposed(st, k + 1)
                    add_outputs(st, k, 2)
                    if more:
                        scores(st, k + 1, 0)
                    add_outputs(st, k, 3)
                    if full and more2:
                        score_maxes(st, k + 2, 0)
                    out_transposed(st, k)
                    if pair_after:
                        if full:
                            wait(pe, s_v, st.batch(2 * (j + 1)))
                        transposes(st, j + 2)
                    if more:
                        scores(st, k + 1, 1)
                    if full and more2:
                        score_maxes(st, k + 2, 1)
                    if full and pair_after:
                        qk_products(st, j + 2)
                    if full and next_pair:
                        wait(pe, s_qk, st.pair(j + (1 if last else 2)) + (1 - NPAIR))
                        v_products(st, j + 1)
                    if layer == FFN:
                        attention_transposed(st, k)
                    if full and more2:
                        score_maxes(st, k + 2, 2)
                    if full:
                        out_projected(st, k)

                steps(pe, layer, slot)

            pe.wait_ge(s_v, 3 * B)
            pe.wait_ge(s_res, 3 * B + RES_CREDIT)
            with pe.Fori(0, NPAIR // 2) as t:
                for i in range(2):
                    pe.wait_ge(s_xn, t * 4 + (3 * B + 2 + 2 * i))
                    pe.wait_ge(s_hn2, t * 2 + (i + HN2_CREDIT))
                    for s in range(2):
                        last = tr(pb[:, s * S:(s + 1) * S], xn[:, i, s, :])
                    last.then_inc(s_t, 1)
            pe.wait_ge(s_hn2, NPAIR + HN2_CREDIT)
            for n in range(B):
                last = mm(fb[:, n * E:(n + 1) * E], hn2T[:, n * S:(n + 1) * S], gate_w[:])
            last.then_inc(s_g, 1)

            pe.wait_ge(s_onehot, 1)
            mm(fb[:, 0:B * E], before[:], onehot[:].rearrange("p b e -> p (b e)"))
            mm(fb[:, B * E:2 * B * E], ones[:], onehot[:].rearrange("p b e -> p (b e)")).then_inc(s_rank, 1)

            def expert(i):
                return pe.value_load(tile_expert_i[0:1, i:i + 1] if isinstance(i, int)
                                     else tile_expert_i[0:1, bass.ds(i, 1)], min_val=0, max_val=E - 1)

            def tile_transposed(i, k):
                wait(pe, s_values[k % TBUF], (i - k % TBUF) * (16 // TBUF) + 16)
                wait(pe, s_tT, i - 1)
                tr((pb, fb)[k % 2][:, 0:S], tile_xn[:, k % TBUF, :]).then_inc(s_xT, 1)

            def hidden(i, k):
                e = expert(i)
                wait(pe, s_tT, i + 1)
                wait(pe, s_mid2, i - 1)
                mm(sbk[k % 2][:], hn2T_tile[:, k % 2, :], w1[:, bass.ds(e, 1), :].rearrange("p o f -> p (o f)")).then_inc(s_up, 1)

            def hidden_transposed(i, k):
                wait(pe, s_mid2, i + 1)
                wait(pe, s_midT, i + (1 - 2 + MIDT_CREDIT))
                for c in range(FC):
                    last = tr(mbk[k % 2][:, c * S:(c + 1) * S], mid[:, k % 2, c * 128:(c + 1) * 128])
                last.then_inc(s_midp, 1)

            def expert_output(i, k):
                e = expert(i)
                wait(pe, s_midT, i + (1 + MIDT_CREDIT))
                wait(pe, s_moe_out, i + (1 - 2 + SUM_CREDIT))
                for c in range(FC):
                    last = mm(obk[k % 2][:, 0:D], midT[:, k % 2, c * S:(c + 1) * S],
                              w2[:, bass.ds(e, 1), c, :].rearrange("p o d -> p (o d)"), start=c == 0, stop=c == FC - 1)
                last.then_inc(s_dn, 1)

            pe.wait_ge(s_moe, 64)
            pe.wait_ge(s_route, 1)
            tile_transposed(0, 0)
            tile_transposed(1, 1)
            hidden(0, 0)

            def expert_slot(s, k):
                if due(s, k, 1):
                    hidden(s + 1, k + 1)
                if due(s, k, 0):
                    hidden_transposed(s, k)
                if due(s, k, 2):
                    tile_transposed(s + 2, k + 2)
                if due(s, k, -1):
                    expert_output(s - 1, k - 1)

            tile_slots(pe, expert_slot)

        @block.scalar
        def _(act):
            def take_hT(st, j):
                i = j % 2
                wait(act, s_t, st.pair(j) + 1)
                wait(act, s_vp, st.pair(j) - NPAIR - 1)
                if st.layer == CROSS:
                    nc.scalar.copy(hT[:, i, :, :].rearrange("p a k -> p (a k)"), pb[:]).then_inc(s_hT, 1)
                else:
                    nc.scalar.activation(hT[:, i, 0, :], pb[:, 0:PAIR], ACT.Identity,
                                         bias=cols[:, 5:6], scale=cols[:, 4:5]).then_inc(s_hT, 1)

            def take_qk(st, j):
                wait(act, s_qkp, st.pair(j) + 1 - NPAIR)
                wait(act, s_r1, st.pair(j))
                if st.layer == CROSS:
                    nc.scalar.activation(qk[:, 0, :], pb[:, 0:PAIR], ACT.Identity, bias=xbq_scaled[:], scale=SCALE)
                    nc.scalar.activation(qk[:, 1, :], pb[:, PAIR:2 * PAIR], ACT.Identity,
                                         bias=cols[:, 1:2], scale=1.0).then_inc(s_qk, 1)
                else:
                    nc.scalar.activation(qk[:, 0, :], pb[:, 0:PAIR], ACT.Identity, bias=cols[:, 2:3], scale=1.0)
                    nc.scalar.activation(qk[:, 1, :], pb[:, PAIR:2 * PAIR], ACT.Identity,
                                         bias=cols[:, 3:4], scale=1.0).then_inc(s_qk, 1)

            def high_parts(st, j, writes):
                i = j % 2
                wait(act, s_wr[i], writes)
                if st.layer == SELF:
                    wait(act, s_t, st.pair(j) + 1)
                    nc.scalar.copy(parts[:, i, 0, 0, :], pb[:, 0:PAIR]).then_inc(s_hi, 1)
                else:
                    wait(act, s_qk, st.pair(j) + 1 - NPAIR)
                    nc.scalar.copy(parts[:, i, 0, :, :], qk[:]).then_inc(s_hi, 1)

            def middle_parts(st, j):
                i, n = j % 2, 1 if st.layer == SELF else 2
                wait(act, s_r1, st.pair(j) + 1)
                nc.scalar.copy(parts[:, i, 1, 0:n, :], rest[:, 0:n, :]).then_inc(s_mid, 1)

            def exponentials(st, k, g):
                wait(act, s_e, st.group(k, g) + 1)
                wait(act, s_pv, st.group(k, g) + (1 - 4 + PV_CREDIT))
                nc.scalar.activation(probs[:, g, :], sbk[g % 2][:], ACT.Exp,
                                     scale=1.0 if st.layer == CROSS else SCALE).then_inc(s_p, 1)

            def take_out(st, k):
                wait(act, s_pv, st.group(k, NG) + PV_CREDIT)
                wait(act, s_otr, st.batch(k) + (1 - 2 + OTR_CREDIT))
                nc.scalar.copy(outT[:, k % 2, :], obk[k % 2][:]).then_inc(s_oevac, 1)

            def take_attT(st, k):
                wait(act, s_atr, st.batch(k) + (1 - 2 * B))
                nc.scalar.copy(attT[:], fb[:, 0:S]).then_inc(s_attT, 1)

            act.sem_inc(s_p, P_CREDIT)
            act.sem_inc(s_oevac, OEV_CREDIT)
            act.sem_inc(s_copied, COPY_CREDIT)
            act.sem_inc(s_hn2, HN2_CREDIT)
            act.sem_inc(s_midT, MIDT_CREDIT)
            act.wait_ge(s_dve_const, 5)
            for layer in (SELF, CROSS, FFN):
                z = Step(act, layer, 0)
                full = layer != SELF
                for j in range(2):
                    if full:
                        take_hT(z, j)
                        take_qk(z, j)
                    high_parts(z, j, z.turn(j) * WRITES)
                    middle_parts(z, j)

                for g in range(NG // 2):
                    exponentials(z, 0, g)

                def slot(st, k, last):
                    j = k // 2
                    more = not (last and k >= UNROLL - 1)
                    pair_after = k % 2 == 0 and not last
                    parts_due = k % 2 == 1 and not last
                    exponentials(st, k, 2)
                    exponentials(st, k, 3)
                    if parts_due:
                        middle_parts(st, j + 2)
                    if more:
                        exponentials(st, k + 1, 0)
                    take_out(st, k)
                    if pair_after:
                        if full:
                            take_hT(st, j + 2)
                        else:
                            high_parts(st, j + 2, st.turn(j + 2) * WRITES)
                    if more:
                        exponentials(st, k + 1, 1)
                    if layer == FFN:
                        take_attT(st, k)
                    if pair_after and full:
                        take_qk(st, j + 2)
                        high_parts(st, j + 2, st.turn(j + 2) * WRITES)

                steps(act, layer, slot)

            act.wait_ge(s_e, 2 * B * NG)
            with act.Fori(0, NPAIR // 2) as t:
                for i in range(2):
                    n = act.snap(t * 2 + i)
                    act.wait_ge(s_xn, n * 2 + (3 * B + 2))
                    nc.scalar.copy(rows_out[:, bass.ds(n * 2, 2), 0:D], xn[:, i, :, :]).then_inc(s_copied, 1)
                    act.wait_ge(s_t, n + (3 * NPAIR + 1))
                    nc.scalar.activation(hn2T[:, bass.ds(n * PAIR, PAIR)], pb[:, 0:PAIR], ACT.Identity,
                                         bias=cols[:, 7:8], scale=cols[:, 6:7]).then_inc(s_hn2, 1)

            def take_tile(i, k):
                act.wait_ge(s_xT, i + 1)
                wait(act, s_up, i - 1)
                nc.scalar.activation(hn2T_tile[:, k % 2, :], (pb, fb)[k % 2][:, 0:S], ACT.Identity,
                                     bias=cols[:, 7:8], scale=cols[:, 6:7]).then_inc(s_tT, 1)

            def rectify(i, k):
                act.wait_ge(s_midp, i + 1)
                wait(act, s_dn, i + (1 - 2 + DN_CREDIT))
                nc.scalar.activation(midT[:, k % 2, :], mbk[k % 2][:], ACT.Relu).then_inc(s_midT, 1)

            take_tile(0, 0)
            take_tile(1, 1)

            def expert_slot(s, k):
                if due(s, k, 0):
                    rectify(s, k)
                if due(s, k, 2):
                    take_tile(s + 2, k + 2)

            tile_slots(act, expert_slot)

        @block.vector
        def _(dve):
            nc.vector.memset(stack[64:KROWS, :, :, :, :], 0.0).then_inc(s_dve_const, 1)
            nc.vector.memset(vaug[:], 0.0).then_inc(s_chain, 1)
            dve.wait_ge(s_chain, 1)
            nc.vector.memset(vaug[:, :, :, HD:HD + 1], 1.0).then_inc(s_dve_const, 1)
            nc.vector.memset(maxparts[:], 0.0).then_inc(s_dve_const, 1)
            nc.vector.memset(ones[:], 1.0).then_inc(s_chain, 1)
            nc.vector.memset(prefix[:], 0.0).then_inc(s_chain, 1)
            nc.vector.memset(starts[:], 0.0).then_inc(s_chain, 1)
            dve.wait_ge(s_pool_const, 6)
            nc.vector.tensor_copy(identb[:], ident[:]).then_inc(s_dve_const, 1)
            dve.wait_ge(s_w, 16 * 15)
            nc.vector.tensor_scalar(xbq_scaled[:], cols[:, 0:1], SCALE, None, ALU.mult).then_inc(s_dve_const, 1)
            dve.sem_inc(s_res, RES_CREDIT)
            dve.sem_inc(s_mfree, MFREE_CREDIT)
            dve.sem_inc(s_moe_out, SUM_CREDIT)
            dve.sem_inc(s_sum, SUM_CREDIT)
            dve.wait_ge(s_x, 32)

            def norm_no(st, j):
                return st.pair(j) if st.layer < FFN else (st.t * 4 + (2 * NPAIR + 2 * j))

            def row_stats(src, no):
                wait(dve, s_rstd, no, s_apart_dve)
                for s in range(2):
                    last = nc.vector.bn_stats(stats[:, s, :], src(s))
                last.then_inc(s_stats, 1)
                wait(dve, s_stats, no + 1, s_apart_dve)
                for s in range(2):
                    nc.vector.bn_aggr(meanvar[:, s, :], stats[:, s, :]).then_inc(s_mv, 1)

            def normalise(dst, src, no, sem_done):
                wait(dve, s_mv, no * 2 + 2)
                wait(dve, s_rstd, no + 1)
                for s in range(2):
                    nc.vector.tensor_scalar(dst(s), src(s), meanvar[:, s, 0:1], rstd[:, s:s + 1],
                                            ALU.subtract, ALU.mult).then_inc(sem_done, 1)

            def x_rows(st, j):
                return lambda s: x_sb[:, st.first + (2 * j + s), :]

            def y_rows(st, j):
                return lambda s: y_sb[:, st.first + (2 * j + s), :]

            def xn_rows(j, layer=FFN):
                if layer == SELF:
                    return lambda s: xn[:, j % 2, s, :].rearrange("p (d h) -> p h d", d=HD)
                return lambda s: xn[:, j % 2, s, :]

            def norm_stats(st, j):
                row_stats(x_rows(st, j), norm_no(st, j))

            def norm_between(st, j):
                if st.layer == FFN:
                    no = norm_no(st, j)
                    normalise(y_rows(st, j), x_rows(st, j), no, s_y)
                    wait(dve, s_y, st.first + (2 * j + 2))
                    row_stats(y_rows(st, j), no + 1)

            def norm_rows(st, j):
                no = norm_no(st, j) + (1 if st.layer == FFN else 0)
                src = y_rows(st, j) if st.layer == FFN else x_rows(st, j)
                wait(dve, s_t, st.pair(j) - 1)
                if st.layer == SELF:
                    wait(dve, s_v, (st.pair(j) - 1) * 2)
                if st.layer == SELF:
                    rows_in = src
                    src = lambda s: rows_in(s).rearrange("p (h d) -> p h d", d=HD)
                normalise(xn_rows(j, st.layer), src, no, s_xn)

            def first_rest(st, j):
                i = j % 2
                wait(dve, s_hi, st.pair(j) + 1)
                wait(dve, s_lo, st.pair(j))
                if st.layer == SELF:
                    nc.vector.tensor_tensor(rest[:, 0, :], pb[:, 0:PAIR], parts[:, i, 0, 0, :],
                                            ALU.subtract).then_inc(s_r1, 1)
                else:
                    nc.vector.tensor_tensor(rest[:], qk[:], parts[:, i, 0, :, :], ALU.subtract).then_inc(s_r1, 1)

            def take_values(st, j):
                wait(dve, s_vp, st.pair(j) + 1 - NPAIR)
                wait(dve, s_pv, (st.pair(j) * 2 - 2) * NG + PV_CREDIT)
                row = rows[:, 0 if st.layer == CROSS else 2, :]
                for s in range(2):
                    nc.vector.tensor_tensor(vaug[:, (2 * j + s) % UNROLL, :, 0:HD],
                                            pb[:, s * S:(s + 1) * S].rearrange("p (h d) -> p h d", d=HD),
                                            row.rearrange("p (h d) -> p h d", d=HD), ALU.add).then_inc(s_v, 1)

            def row_maxes(st, k, g):
                bank = mbk[(k * PERM_M + g) % 2]
                if st.layer == CROSS and g == 0:
                    wait(dve, s_bias[k % 4], (st.t + k // 4) * 32 + 32)
                wait(dve, s_mp, st.maxuse(k, g) + 1, s_apart_dve)
                if st.layer == CROSS:
                    for h in range(G):
                        head = g * G + h
                        last = nc.vector.tensor_tensor_reduce(
                            out=bank[:, h * S:(h + 1) * S], in0=bank[:, h * S:(h + 1) * S], in1=bias_in[:, k % 4, head, :], scale=1.0,
                            scalar=-3.0e38, op0=ALU.add, op1=ALU.max, accum_out=rowmax[:, head:head + 1])
                else:
                    last = nc.vector.tensor_reduce(rowmax[:, g * G:(g + 1) * G],
                                                   bank[:].rearrange("p (h k) -> p h k", h=G), AX.X, ALU.max)
                last.then_inc(s_mfree, 1)

            def max_parts(st, k):
                wait(dve, s_mfree, st.maxuse(k, NG) + MFREE_CREDIT)
                nc.vector.tensor_scalar(maxparts[:, 0:NH], rowmax[:], -1.0, None, ALU.mult).then_inc(s_mhi, 1)
                wait(dve, s_mhi, st.batch(k) + (1 - B))
                nc.vector.scalar_tensor_tensor(out=maxparts[:, NH:2 * NH], in0=rowmax[:], scalar=-1.0,
                                               in1=maxparts[:, 0:NH], op0=ALU.mult,
                                               op1=ALU.subtract).then_inc(s_mparts, 1)

            def take_maxT(st, k):
                wait(dve, s_mp, st.maxuse(k, NG) + 1)
                wait(dve, s_e, (st.batch(k) - 1) * NG)
                nc.vector.tensor_copy(maxT[:, k % 2, :],
                                      mbk[(k * PERM_M + NG) % 2][:].bitcast(bf16)[:, 0:128]).then_inc(s_mfree, 1)

            def attention(st, k):
                wait(dve, s_otr, st.batch(k) + (1 + OTR_CREDIT))
                o = fb[:].rearrange("p (h c) -> p h c", c=VC)
                nc.vector.reciprocal(rowsum_inv[:], o[:, :, HD]).then_inc(s_inv, 1)
                wait(dve, s_inv, st.batch(k) + 1)
                if st.layer == CROSS:
                    nc.vector.tensor_tensor(inv_sel[:], rowsum_inv[:].unsqueeze(2).to_broadcast([128, NH, TQ]),
                                            in_block[:].unsqueeze(1).to_broadcast([128, NH, TQ]),
                                            ALU.mult).then_inc(s_invsel, 1)
                    wait(dve, s_invsel, st.batch(k) + (1 - B))
                    nc.vector.tensor_tensor(
                        att_sel[:], o[:, :, 0:HD].rearrange("p h d -> p d h").unsqueeze(3).to_broadcast([128, HD, NH, TQ]),
                        inv_sel[:].unsqueeze(1).to_broadcast([128, HD, NH, TQ]), ALU.mult).then_inc(s_att, 1)
                    return
                nc.vector.tensor_tensor(att[:].rearrange("p (h d) -> p h d", d=HD), o[:, :, 0:HD],
                                        rowsum_inv[:].unsqueeze(2).to_broadcast([128, NH, HD]),
                                        ALU.mult).then_inc(s_att, 1)
                if st.layer == SELF:
                    wait(dve, s_att, st.batch(k) + 1)
                    r = x_sb[:, st.first + k, :]
                    nc.vector.tensor_tensor(r, r, att[:], ALU.add).then_inc(s_res, 1)

            def residual(st, k):
                res = x_sb if st.layer == CROSS else y_sb
                if k % 2 == 0:
                    wait(dve, s_resbias, st.pair(k // 2) + (1 - NPAIR))
                wait(dve, s_oproj, st.batch(k) + (1 - B))
                r = res[:, st.first + k, :]
                nc.vector.tensor_tensor(r, fb[:, 0:D], r, ALU.add).then_inc(s_res, 1)

            for layer in (SELF, CROSS, FFN):
                z = Step(dve, layer, 0)
                full = layer != SELF
                if layer != SELF:
                    wait(dve, s_res, B * layer + RES_CREDIT)
                for j in range(2):
                    norm_stats(z, j)
                    norm_between(z, j)
                    norm_rows(z, j)
                    first_rest(z, j)
                    if full and j == 0:
                        take_values(z, 0)
                if full:
                    for g in range(NG):
                        row_maxes(z, 0, g)
                    max_parts(z, 0)
                    take_maxT(z, 0)
                    for g in range(NG - 1):
                        row_maxes(z, 1, g)

                def slot(st, k, last):
                    j = k // 2
                    more = not (last and k >= UNROLL - 1)
                    more2 = not (last and k >= UNROLL - 2)
                    next_pair = k % 2 == 1 and not (last and j == 1)
                    pair_after = k % 2 == 0 and not last
                    rest_due = k % 2 == 1 and not last
                    if pair_after:
                        norm_stats(st, j + 2)
                    if full and more:
                        row_maxes(st, k + 1, 3)
                        max_parts(st, k + 1)
                    if rest_due:
                        first_rest(st, j + 2)
                    if full and more:
                        take_maxT(st, k + 1)
                    if pair_after:
                        norm_between(st, j + 2)
                        if layer != FFN:
                            norm_rows(st, j + 2)
                    if full and more2:
                        row_maxes(st, k + 2, 0)
                    if pair_after and layer == FFN:
                        norm_rows(st, j + 2)
                    attention(st, k)
                    if full and more2:
                        row_maxes(st, k + 2, 1)
                    if full and next_pair:
                        take_values(st, j + 1)
                    if full and more2:
                        row_maxes(st, k + 2, 2)
                    if full:
                        residual(st, k)

                steps(dve, layer, slot)

            dve.wait_ge(s_res, 3 * B + RES_CREDIT)
            with dve.Fori(0, NPAIR // 2) as t:
                for i in range(2):
                    n = dve.snap(t * 2 + i)
                    rows_of = lambda s: y_sb[:, n * 2 + s, :]
                    row_stats(rows_of, n + 4 * NPAIR)
                    dve.wait_ge(s_t, n + (3 * NPAIR - 1))
                    dve.wait_ge(s_copied, n + (1 - 2 + COPY_CREDIT))
                    normalise(xn_rows(i), rows_of, n + 4 * NPAIR, s_xn)

            chain = [4]

            def link(ins):
                chain[0] += 1
                ins.then_inc(s_chain, 1)
                dve.wait_ge(s_chain, chain[0])

            over_b = lambda t: t.unsqueeze(1).to_broadcast([128, B, E])
            over_e = lambda t: t.unsqueeze(2).to_broadcast([128, B, E])
            dve.wait_ge(s_g, 1)
            link(nc.vector.tensor_tensor(logits[:], fb[:, 0:B * E].rearrange("p (b e) -> p b e", e=E),
                                         over_b(gate_b[:]), ALU.add))
            link(nc.vector.tensor_reduce(best[:], logits[:], AX.X, ALU.max))
            link(nc.vector.tensor_tensor(is_best[:], logits[:], over_e(best[:]), ALU.is_equal))
            link(nc.vector.scalar_tensor_tensor(out=place[:], in0=is_best[:], scalar=-float(E), in1=over_b(expert_no[:]),
                                                op0=ALU.mult, op1=ALU.add))
            link(nc.vector.tensor_reduce(first_best[:], place[:], AX.X, ALU.min))
            nc.vector.scalar_tensor_tensor(
                out=onehot[:], in0=over_e(first_best[:]), scalar=float(E), in1=over_b(expert_no[:]),
                op0=ALU.add, op1=ALU.is_equal).then_inc(s_onehot, 1)

            dve.wait_ge(s_rank, 1)
            half_b, half_e = B // 2, E // 2
            link(nc.vector.tensor_copy(prefix[:, 0, half_b:, :],
                                       fb[:, B * E:2 * B * E].rearrange("p (b e) -> p b e", e=E)))
            i, step = 0, 1
            while step < B:
                link(nc.vector.tensor_tensor(prefix[:, 1 - i, half_b:, :], prefix[:, i, half_b:, :],
                                             prefix[:, i, half_b - step:half_b - step + B, :], ALU.add))
                i, step = 1 - i, step * 2
            link(nc.vector.tensor_tensor(over_end[:], prefix[:, i, half_b + B - 1, :].unsqueeze(2).to_broadcast([128, E, B]),
                                         tile_ends[:].unsqueeze(1).to_broadcast([128, E, B]), ALU.is_gt))
            link(nc.vector.tensor_reduce(starts[:, 0, half_e:], over_end[:], AX.X, ALU.add))
            j, step = 0, 1
            while step < E:
                link(nc.vector.tensor_tensor(starts[:, 1 - j, half_e:], starts[:, j, half_e:],
                                             starts[:, j, half_e - step:half_e - step + E], ALU.add))
                j, step = 1 - j, step * 2
            start = starts[:, j, half_e - 1:half_e - 1 + E]
            link(nc.vector.tensor_tensor(place_in[:], fb[:, 0:B * E].rearrange("p (b e) -> p b e", e=E),
                                         prefix[:, i, half_b - 1:half_b - 1 + B, :], ALU.add))
            link(nc.vector.scalar_tensor_tensor(out=place[:], in0=over_b(start), scalar=float(TILE), in1=place_in[:],
                                                op0=ALU.mult, op1=ALU.add))
            link(nc.vector.tensor_tensor(place_in[:], place[:], onehot[:], ALU.mult))
            link(nc.vector.tensor_reduce(position[:], place_in[:], AX.X, ALU.add))
            link(nc.vector.tensor_copy(position_i[:], position[:]))
            link(nc.vector.tensor_tensor(started[:], tile_no[0:1, :].unsqueeze(2).to_broadcast([1, NTILES, E]),
                                         starts[0:1, j, half_e - 1:half_e - 1 + E].unsqueeze(1).to_broadcast([1, NTILES, E]),
                                         ALU.is_ge))
            link(nc.vector.tensor_reduce(tile_expert[:], started[:], AX.X, ALU.add))
            nc.vector.tensor_scalar(tile_expert_i[:], tile_expert[:], -1.0, None, ALU.add).then_inc(s_route, 1)
            dve.wait_ge(s_route, 1)
            dve.wait_ge(s_moe, 64)

            def expert(i):
                return dve.value_load(tile_expert_i[0:1, i:i + 1] if isinstance(i, int)
                                      else tile_expert_i[0:1, bass.ds(i, 1)], min_val=0, max_val=E - 1)

            def hidden_biased(i, k):
                e = expert(i)
                dve.wait_ge(s_up, i + 1)
                wait(dve, s_midp, i - 1)
                nc.vector.tensor_tensor(mid[:, k % 2, :], sbk[k % 2][:],
                                        b1_rows[:, bass.ds(e, 1), :].rearrange("p o f -> p (o f)"),
                                        ALU.add).then_inc(s_mid2, 1)

            def tile_summed(i, k):
                e = expert(i)
                dve.wait_ge(s_dn, i + (1 + DN_CREDIT))
                wait(dve, s_sum, i + (1 - 2 + SUM_CREDIT))
                nc.vector.tensor_tensor(moe[:, k % 2, :], obk[k % 2][:, 0:D],
                                        b2_rows[:, bass.ds(e, 1), :].rearrange("p o d -> p (o d)"),
                                        ALU.add).then_inc(s_moe_out, 1)
                dve.wait_ge(s_moe_out, i + (1 + SUM_CREDIT))
                dve.wait_ge(s_residuals[k % TBUF], (i - k % TBUF) * (16 // TBUF) + 16)
                r = tile_res[:, k % TBUF, 0:D]
                nc.vector.tensor_tensor(r, r, moe[:, k % 2, :], ALU.add).then_inc(s_sum, 1)

            hidden_biased(0, 0)

            def expert_slot(s, k):
                if due(s, k, 1):
                    hidden_biased(s + 1, k + 1)
                if due(s, k, -1):
                    tile_summed(s - 1, k - 1)

            tile_slots(dve, expert_slot)


def kernel(**inputs):
    import concourse.bacc as bacc
    from concourse.bass_utils import run_bass_kernel_spmd

    g = {k: np.ascontiguousarray(v) for k, v in inputs.items()}
    x_ = lambda n: g["L0_xattn_" + n]
    f_ = lambda n: g["L0_ffn_" + n]
    by_feature = lambda v: v.reshape(-1, NH, HD).swapaxes(1, 2).reshape(v.shape)
    arrays = {
        "x": g["x"], "ctx": g["ctx_1024"], "bias": g["fside_Bx16xSxS2_0"],
        "w_xq": by_feature(x_("Wq").T), "w_xk": by_feature(x_("Wk").T), "w_xv": x_("Wv").T, "w_xo": x_("Wo").T,
        "w_fq": by_feature(f_("wq")), "w_fk": by_feature(f_("wk")), "w_fv": f_("wv"), "w_fo": f_("wo"),
        "cols": np.stack([by_feature(x_("bq")), by_feature(x_("bk")), by_feature(f_("bq")), by_feature(f_("bk")), f_("ln1_g"), f_("ln1_b"),
                          f_("ln2_g"), f_("ln2_b")], axis=1),
        "xbv": x_("bv"), "xbo": x_("bo"), "fbv": f_("bv"), "fbo": f_("bo"),
        "gate_w": f_("gate_w"), "gate_b": f_("gate_b"), "w1": f_("w1"), "w2": f_("w2"),
        "b1": f_("b1"), "b2": f_("b2"),
    }
    arrays = {k: np.ascontiguousarray(v) for k, v in arrays.items()}
    nc = bacc.Bacc("TRN2", target_bir_lowering=False, num_devices=1)
    aps = {k: nc.dram_tensor("in_" + k, v.shape, mybir.dt.from_np(v.dtype), kind="ExternalInput").ap()
           for k, v in arrays.items()}
    out = nc.dram_tensor("out", (B, S, D), mybir.dt.float32, kind="ExternalOutput").ap()
    build(nc, aps, out)
    r = run_bass_kernel_spmd(nc, [{"in_" + k: v for k, v in arrays.items()}], core_ids=[0])
    return r.results[0]["out"]
```

```python
import numpy as np
from contextlib import ExitStack

import concourse.bass as bass
from concourse import mybir

B, S, D = 16, 128, 128
NH, HD = 16, 8
E, F = 8, 512
FC = F // 128
EPS = 1e-5
SCALE = HD ** -0.5
G = 4
NG = NH // G
PAIR = 2 * S
NPAIR = B // 2
UNROLL = 4
NT = 3
ROWS = NT * NT * HD
KROWS = 96
VC = 32
MASKED = -1e30
TR = D // HD
TQ = S // TR

TILE = 128
NTILES = B * S // TILE + E - 1
TBUF = 4
WIDTH = 2 * D + 1

SELF, CROSS, FFN = 0, 1, 2
PERM_M = NG + 1


def wait(eng, sem, value, apart=None):
    if not isinstance(value, int) or value > 0:
        eng.wait_ge(sem, value)
        if apart is not None and not isinstance(value, int):
            eng.sem_inc(apart, 1)


class Step:

    def __init__(self, eng, layer, t):
        fixed = isinstance(t, int)
        snap = (lambda v: v) if fixed else eng.snap
        self.layer, self.t = layer, t
        self.first = snap(t * UNROLL)
        self.groups = snap(t * (UNROLL * NG))
        self.maxes = snap(t * (UNROLL * PERM_M))

    def batch(self, k):
        return self.first + (B * self.layer + k)

    def group(self, k, g):
        return self.groups + (B * NG * self.layer + k * NG + g)

    def maxuse(self, k, g):
        return self.maxes + (B * PERM_M * (self.layer - 1) + k * PERM_M + g)

    def pair(self, j):
        return self.t * 2 + (NPAIR * self.layer + j)

    def turn(self, j):
        return self.t + (NPAIR // 2 * self.layer + j // 2)


def ahead(eng, st, j, last, count):
    if not last or j < count:
        return st, j
    return (Step(eng, st.layer + 1, 0), j - count) if st.layer < FFN else None


LAST_NORMS = [(0, 1), (2,), (3, 4), (5, 6)]
LEFT = NPAIR - 1


def last_norms(st, k, last):
    pairs = LAST_NORMS[k] if st.layer == FFN and last else ()
    return pairs[:1], pairs[1:]


def build(nc, a, out):
    f32, bf16, i32 = mybir.dt.float32, mybir.dt.bfloat16, mybir.dt.int32
    ALU, ACT, AX = mybir.AluOpType, mybir.ActivationFunctionType, mybir.AxisListType

    ctx = ExitStack()
    with ctx:
        def sb(name, shape, dt=f32):
            return ctx.enter_context(nc.sbuf_tensor(name, shape, dt))

        def sem(name):
            return ctx.enter_context(nc.semaphore(name))

        x_sb = sb("x_sb", [128, B, D])
        y_sb = sb("y_sb", [128, B, D])
        xn = sb("xn", [128, 2, 2, D])
        stats = sb("stats", [128, 2, 6])
        meanvar = sb("meanvar", [128, 2, 2])
        vareps = sb("vareps", [128, 2])
        rstd = sb("rstd", [128, 2])
        ctx_in = sb("ctx_in", [128, 2, 2, D])
        hT = sb("hT", [128, 2, 2, PAIR])
        qk = sb("qk", [128, 2, PAIR])
        rest = sb("rest", [128, 2, PAIR])
        parts = sb("parts", [128, 2, NT, 2, PAIR], bf16)
        stack = sb("stack", [KROWS, 2, 2, NH, PAIR], bf16)
        vaug = sb("vaug", [128, UNROLL, NH, VC])
        bias_in = sb("bias_in", [128, 4, NH, S])
        rows_out = bias_in[:].rearrange("p a h k -> p (a h k)")[:, 0:B * WIDTH].rearrange("p (b w) -> p b w", w=WIDTH)
        probs = sb("probs", [128, NG, G * S])
        rowmax = sb("rowmax", [128, NH])
        maxparts = sb("maxparts", [128, 128], bf16)
        maxT = sb("maxT", [128, 2, 128], bf16)
        outT = sb("outT", [128, 2, NG * S])
        rowsum_inv = sb("rowsum_inv", [128, NH])
        att = sb("att", [128, D])
        attT = sb("attT", [128, S])
        ident = sb("ident", [128, 128])
        identb = sb("identb", [128, 128], bf16)
        causal = sb("causal", [128, S], bf16)
        pick = sb("pick", [128, NH, S], bf16)
        zero = sb("zero", [128, 1])
        minus_half = sb("minus_half", [128, 2])
        in_block = sb("in_block", [128, TQ])
        inv_sel = sb("inv_sel", [128, NH, TQ])
        att_sel = sb("att_sel", [128, HD, NH, TQ])
        wxo = sb("wxo", [128, HD, D])
        wx = {k: sb("w_" + k, [128, D]) for k in ("xq", "xk", "xv", "fq", "fk", "fv", "fo")}
        cols = sb("cols", [128, 8])
        xbq_scaled = sb("xbq_scaled", [128, 1])
        rows = sb("rows", [128, 4, D])
        gate_w = sb("gate_w", [128, E])
        gate_b = sb("gate_b", [128, E])
        w1 = sb("w1", [128, E, F])
        w2 = sb("w2", [128, E, FC, D])
        b1_rows = sb("b1_rows", [128, E, F])
        b2_rows = sb("b2_rows", [128, E, D])
        hn2T = sb("hn2T", [128, B * S])
        logits = sb("logits", [128, B, E])
        best = sb("best", [128, B])
        is_best = sb("is_best", [128, B, E])
        expert_no = sb("expert_no", [128, E])
        place = sb("place", [128, B, E])
        first_best = sb("first_best", [128, B])
        onehot = sb("onehot", [128, B, E])
        before = sb("before", [128, 128])
        ones = sb("ones", [128, 128])
        prefix = sb("prefix", [128, 2, B // 2 + B, E])
        tile_ends = sb("tile_ends", [128, B])
        over_end = sb("over_end", [128, E, B])
        starts = sb("starts", [128, 2, E // 2 + E])
        place_in = sb("place_in", [128, B, E])
        position = sb("position", [128, B])
        position_i = sb("position_i", [128, B], i32)
        tile_no = sb("tile_no", [128, NTILES])
        started = sb("started", [1, NTILES, E])
        tile_expert = sb("tile_expert", [1, NTILES])
        tile_expert_i = sb("tile_expert_i", [1, NTILES], i32)
        filler = sb("filler", [128, WIDTH])
        tile_xn = outT[:].rearrange("p b (t d) -> p (b t) d", d=D)[:, 0:TBUF, :]
        tile_res = vaug[:].rearrange("p b h c -> p (b h c)")[:, 0:TBUF * (WIDTH - D)].rearrange(
            "p (b w) -> p b w", w=WIDTH - D)
        hn2T_tile, moe = xn[:, 0, :, :], xn[:, 1, :, :]
        mid, midT = probs[:, 0:2, :], probs[:, 2:4, :]

        def stack_tail(i):
            return stack[64:KROWS, i, :, :, :].rearrange("p w h k -> p (w h k)").bitcast(f32)

        pb = ctx.enter_context(nc.psum_tensor("prep_bank", [128, 512], f32))
        fb = ctx.enter_context(nc.psum_tensor("finish_bank", [128, 512], f32))
        sbk = [ctx.enter_context(nc.psum_tensor(f"score_bank{i}", [128, G * S], f32)) for i in range(2)]
        mbk = [ctx.enter_context(nc.psum_tensor(f"max_bank{i}", [128, G * S], f32)) for i in range(2)]
        obk = [ctx.enter_context(nc.psum_tensor(f"out_bank{i}", [128, NG * S], f32)) for i in range(2)]

        scratch = nc.dram_tensor("parts_scratch", (2, 2, NT, HD, NH, PAIR), bf16, kind="Internal").ap()
        row_elems = NH * PAIR
        routed = nc.dram_tensor("routed_rows", (NTILES * TILE, WIDTH), f32, kind="Internal").ap()

        WRITES, READS = 2 * 16, (NT + 1) * 16

        s_apart_dve = sem("waited_apart_dve")
        s_apart_pool = sem("waited_apart_pool")
        s_x = [sem("first_x_loaded"), sem("x_loaded")]
        s_w = sem("weights_loaded")
        s_moe = sem("expert_weights_loaded")
        s_ctx = [sem(f"ctx_loaded{i}") for i in range(2)]
        s_bias = [sem(f"bias_loaded{i}") for i in range(4)]
        s_wr = [sem(f"scratch_written{i}") for i in range(2)]
        s_stack = [sem(f"stack_loaded{i}") for i in range(2)]
        s_pool_const = sem("pool_constants")
        s_ident = sem("identity_causal_zeros")
        s_dve_const = sem("dve_constants")
        s_zero = [sem(f"stack_zeroed{i}") for i in range(2)]
        s_stats = sem("stats_ready")
        s_mv = sem("meanvar_ready")
        s_ve = sem("vareps_ready")
        s_rstd = sem("rstd_ready")
        s_y = sem("ffn_input_ready")
        s_xn = sem("xn_ready")
        s_t = sem("transposed")
        s_hT = sem("hT_ready")
        s_qkp = sem("qk_products")
        s_qk = sem("qk_ready")
        s_hi = sem("high_parts")
        s_r1 = sem("first_rest")
        s_mid = sem("middle_parts")
        s_lo = sem("low_parts")
        s_resbias = sem("residual_biased")
        s_vp = sem("v_products")
        s_v = sem("v_ready")
        s_mp = sem("max_products")
        s_mfree = sem("max_bank_free")
        s_mhi = sem("max_high_part")
        s_mparts = sem("max_parts")
        s_e = sem("scores_ready")
        s_p = sem("probs_ready")
        s_pv = sem("outputs_added")
        s_oevac = sem("out_copied")
        s_otr = sem("out_transposed")
        s_inv = sem("rowsum_inverted")
        s_invsel = sem("inverse_in_block")
        s_att = sem("attention_ready")
        s_atr = sem("attention_transposed")
        s_attT = sem("attT_ready")
        s_oproj = sem("out_projected")
        s_res = sem("residual_done")
        s_g = sem("gate_products")
        s_hn2 = sem("hn2T_ready")
        s_copied = sem("rows_copied")
        s_rr = sem("rows_summed")
        s_chain = sem("gate_chain")
        s_onehot = sem("choices_ready")
        s_rank = sem("rank_products")
        s_route = sem("positions_ready")
        s_fill = sem("filler_written")
        s_routed = sem("rows_routed")
        s_values = [sem(f"values_loaded{i}") for i in range(TBUF)]
        s_residuals = [sem(f"residuals_loaded{i}") for i in range(TBUF)]
        s_stored = [sem(f"tile_stored{i}") for i in range(TBUF)]
        s_xT = sem("tile_transposed")
        s_tT = sem("hn2T_tile_ready")
        s_up = sem("hidden_products")
        s_mid2 = sem("hidden_biased")
        s_midp = sem("hidden_transposed")
        s_midT = sem("midT_ready")
        s_dn = sem("expert_output")
        s_moe_out = sem("moe_ready")
        s_sum = sem("tile_summed")

        P_CREDIT, PV_CREDIT, OEV_CREDIT, OTR_CREDIT, RES_CREDIT, MFREE_CREDIT = 2, 4, 2, 2, 1, 2
        SUM_CREDIT, MIDT_CREDIT, DN_CREDIT = 2, 1, 1

        block = ctx.enter_context(nc.Block())

        def steps(eng, layer, slot):
            def body(t, last):
                st = Step(eng, layer, t)
                for k in range(UNROLL):
                    slot(st, k, last)
            with eng.Fori(0, B // UNROLL - 1) as t:
                body(t, False)
            body(B // UNROLL - 1, True)

        def tile_slots(eng, slot):
            slot(0, 0)
            with eng.Fori(0, (NTILES - 3) // TBUF) as t:
                for k in range(1, TBUF + 1):
                    slot(eng.snap(t * TBUF + k), k)
            for s in range(NTILES - 2, NTILES + 1):
                slot(s, s)

        def due(s, ahead):
            return 0 <= s + ahead < NTILES if isinstance(s, int) else True

        @block.sync
        def _(sp):
            xr = a["x"].rearrange("b s d -> s b d")
            sp.dma_start(x_sb[:, 0:UNROLL, :], xr[:, 0:UNROLL, :]).then_inc(s_x[0], 16)
            sp.dma_start(x_sb[:, UNROLL:B, :], xr[:, UNROLL:B, :]).then_inc(s_x[1], 16)
            for k in wx:
                sp.dma_start(wx[k][:], a["w_" + k]).then_inc(s_w, 16)
            sp.dma_start(wxo[:].rearrange("p d n -> p (d n)"),
                         bass.AP(tensor=a["w_xo"].tensor, offset=a["w_xo"].offset,
                                 ap=[[0, TQ], [HD * D, TR], [1, HD * D]])).then_inc(s_w, 16)
            sp.dma_start(cols[:], a["cols"]).then_inc(s_w, 16)
            for i, k in enumerate(("xbv", "xbo", "fbv", "fbo")):
                sp.dma_start(rows[:, i, :], a[k].partition_broadcast(128)).then_inc(s_w, 16)
            sp.dma_start(gate_w[:], a["gate_w"]).then_inc(s_w, 16)
            sp.dma_start(gate_b[:], a["gate_b"].partition_broadcast(128)).then_inc(s_w, 16)

            def write_parts(st, j):
                i = j % 2
                wait(sp, s_lo, st.pair(j) + 1)
                wait(sp, s_stack[i], st.turn(j) * READS)
                for w in range(1 if st.layer == SELF else 2):
                    sp.dma_start(scratch[i, w].rearrange("p d h k -> (d h) p k"),
                                 parts[:, i, :, w, :]).then_inc(s_wr[i], 16)
                if st.layer == SELF:
                    sp.sem_inc(s_wr[i], WRITES // 2)

            def read_stack(st, j):
                i = j % 2
                wait(sp, s_wr[i], st.turn(j) * WRITES + WRITES)
                if j > 0 or st.layer != SELF:
                    wait(sp, s_e, st.batch(2 * j - 2) * NG + 1)
                wk = 0 if st.layer == SELF else 1
                for part in range(NT):
                    q_src = bass.AP(tensor=scratch.tensor, offset=scratch[i, 0, part].offset,
                                    ap=[[0, NT], [row_elems, HD], [1, row_elems]])
                    r0 = part * NT * HD
                    sp.dma_start(stack[r0:r0 + NT * HD, i, 0, :, :], q_src).then_inc(s_stack[i], 16)
                k_src = bass.AP(tensor=scratch.tensor, offset=scratch[i, wk].offset,
                                ap=[[0, NT], [row_elems, NT * HD], [1, row_elems]])
                sp.dma_start(stack[0:ROWS, i, 1, :, :], k_src).then_inc(s_stack[i], 16)

            def load_bias(st, k):
                i = k % 4
                if not (isinstance(st.t, int) and st.t == 0 and k < 4):
                    wait(sp, s_e, st.batch(k - 3) * NG)
                src = a["bias"][bass.ds(st.first + k, 1)].rearrange("o h q k -> q (o h) k")
                for half in range(2):
                    heads = slice(half * NH // 2, (half + 1) * NH // 2)
                    sp.dma_start(bias_in[:, i, heads, :], src[:, heads, :]).then_inc(s_bias[i], 16)

            def load_ctx(st, j):
                i = j % 2
                if not (isinstance(st.t, int) and j < 2):
                    wait(sp, s_t, st.pair(j) - 1)
                sp.dma_start(ctx_in[:, i, :, :],
                             a["ctx"][bass.ds(st.first + 2 * j, 2)].rearrange("b s d -> s b d")).then_inc(s_ctx[i], 16)

            z = Step(sp, SELF, 0)
            write_parts(z, 0)
            sp.wait_ge(s_zero[0], 1)
            read_stack(z, 0)
            write_parts(z, 1)
            for i in range(2):
                load_bias(Step(sp, CROSS, 0), i)
            sp.wait_ge(s_zero[1], 1)

            def slot(st, k, last):
                j = k // 2
                pair_next, pair_after = ahead(sp, st, j + 1, last, 2), ahead(sp, st, j + 2, last, 2)
                if st.layer == SELF and last and k == 0:
                    for i in range(2):
                        load_ctx(Step(sp, CROSS, 0), i)
                if st.layer == CROSS and k % 2 == 0 and not last:
                    load_ctx(st, j + 2)
                if k % 2 == 0 and pair_next:
                    read_stack(*pair_next)
                if st.layer == SELF and last and k == 1:
                    load_bias(Step(sp, CROSS, 0), 2)
                if st.layer == CROSS and not (last and k >= 1):
                    load_bias(st, k + 3)
                if k % 2 == 1 and pair_after:
                    write_parts(*pair_after)

            for layer in (SELF, CROSS, FFN):
                steps(sp, layer, slot)

            sp.wait_ge(s_pool_const, 13)
            sp.dma_start(routed.rearrange("(t p) w -> p t w", p=TILE),
                         filler[:].unsqueeze(1).to_broadcast([128, NTILES, WIDTH])).then_inc(s_fill, 16)
            sp.dma_start(w1[:], a["w1"].rearrange("e h f -> h e f")).then_inc(s_moe, 16)
            sp.dma_start(b1_rows[:], a["b1"].partition_broadcast(128)).then_inc(s_moe, 16)
            sp.dma_start(w2[:], a["w2"].rearrange("e (c p) h -> p e c h", p=128)).then_inc(s_moe, 16)
            sp.dma_start(b2_rows[:], a["b2"].partition_broadcast(128)).then_inc(s_moe, 16)

            sp.wait_ge(s_routed, 16 * B)

            def load_values(i, buf):
                wait(sp, s_xT, i + (1 - TBUF))
                sp.dma_start(tile_xn[:, buf, :], routed[bass.ds(i * TILE, TILE), 0:D]).then_inc(s_values[buf], 16)

            def load_residuals(i, buf):
                wait(sp, s_stored[buf], (i - buf) * (16 // TBUF))
                sp.dma_start(tile_res[:, buf, :], routed[bass.ds(i * TILE, TILE), D:WIDTH]).then_inc(s_residuals[buf], 16)

            first = TBUF + 2
            for i in range(first):
                load_values(i, i % TBUF)
                if i >= 2:
                    load_residuals(i - 2, i - 2)
            with sp.Fori(0, (NTILES - first) // TBUF) as t:
                for k in range(TBUF):
                    i = sp.snap(t * TBUF + (first + k))
                    load_values(i, (first + k) % TBUF)
                    load_residuals(i - 2, (first + k - 2) % TBUF)
            for i in range(first + (NTILES - first) // TBUF * TBUF, NTILES + 2):
                if i < NTILES:
                    load_values(i, i % TBUF)
                load_residuals(i - 2, (i - 2) % TBUF)
            for i in range(TBUF):
                sp.wait_ge(s_stored[i], 16 * ((NTILES - 1 - i) // TBUF + 1))

        @block.gpsimd
        def _(pool):
            nc.gpsimd.memset(ident[:], 0.0).then_inc(s_ident, 1)
            nc.gpsimd.memset(causal[:], 0.0).then_inc(s_ident, 1)
            nc.gpsimd.memset(zero[:], 0.0).then_inc(s_ident, 1)
            nc.gpsimd.memset(minus_half[:], -0.5).then_inc(s_ident, 1)
            pool.wait_ge(s_ident, 4)
            nc.gpsimd.affine_select(out=ident[:], in_=ident[:], compare_op=ALU.not_equal, fill=1.0, base=0,
                                    pattern=[[-1, 128]], channel_multiplier=1).then_inc(s_ident, 1)
            nc.gpsimd.affine_select(out=causal[:], in_=causal[:], compare_op=ALU.is_ge, fill=MASKED, base=0,
                                    pattern=[[1, S]], channel_multiplier=-1).then_inc(s_ident, 1)
            nc.gpsimd.memset(pick[:], 0.0).then_inc(s_pool_const, 1)
            nc.gpsimd.memset(in_block[:], 1.0).then_inc(s_pool_const, 1)
            nc.gpsimd.memset(before[:], 1.0).then_inc(s_pool_const, 1)
            nc.gpsimd.memset(filler[:], 0.0).then_inc(s_pool_const, 1)

            def constants_of_layers():
                pool.wait_ge(s_pool_const, 4)
                nc.gpsimd.affine_select(out=pick[:], in_=pick[:], compare_op=ALU.not_equal, fill=1.0, base=0,
                                        pattern=[[-1, NH], [0, S]], channel_multiplier=1).then_inc(s_pool_const, 1)
                nc.gpsimd.affine_select(out=in_block[:], in_=in_block[:], compare_op=ALU.is_ge, fill=0.0, base=0,
                                        pattern=[[-TR, TQ]], channel_multiplier=1).then_inc(s_pool_const, 1)
                nc.gpsimd.affine_select(out=before[:], in_=before[:], compare_op=ALU.is_gt, fill=0.0, base=0,
                                        pattern=[[1, 128]], channel_multiplier=-1).then_inc(s_pool_const, 1)
                pool.wait_ge(s_pool_const, 7)
                nc.gpsimd.affine_select(out=pick[:], in_=pick[:], compare_op=ALU.not_equal, fill=1.0, base=-NH,
                                        pattern=[[-1, NH], [0, S]], channel_multiplier=1).then_inc(s_pool_const, 1)
                nc.gpsimd.affine_select(out=in_block[:], in_=in_block[:], compare_op=ALU.is_ge, fill=0.0, base=TR - 1,
                                        pattern=[[TR, TQ]], channel_multiplier=-1).then_inc(s_pool_const, 1)
                nc.gpsimd.iota(expert_no[:], pattern=[[1, E]], base=0, channel_multiplier=0,
                               allow_small_or_imprecise_dtypes=True).then_inc(s_pool_const, 1)
                nc.gpsimd.iota(tile_ends[:], pattern=[[TILE, B]], base=0, channel_multiplier=0,
                               allow_small_or_imprecise_dtypes=True).then_inc(s_pool_const, 1)
                nc.gpsimd.iota(tile_no[:], pattern=[[1, NTILES]], base=0, channel_multiplier=0,
                               allow_small_or_imprecise_dtypes=True).then_inc(s_pool_const, 1)
                nc.gpsimd.iota(filler[:].bitcast(i32)[:, 2 * D:WIDTH], pattern=[[0, 1]], base=B * S,
                               channel_multiplier=1).then_inc(s_pool_const, 1)

            def inverse_deviation(norm_no):
                wait(pool, s_mv, norm_no * 2 + 2, s_apart_pool)
                nc.gpsimd.tensor_scalar(vareps[:], meanvar[:, :, 1], EPS, None, ALU.add).then_inc(s_ve, 1)
                wait(pool, s_ve, norm_no + 1)
                nc.gpsimd.tensor_tensor(rstd[:], vareps[:], minus_half[:], ALU.pow).then_inc(s_rstd, 1)

            def norm_no(st, j):
                return st.pair(j) if st.layer < FFN else (st.t * 4 + (2 * NPAIR + 2 * j))

            def start_pair(st, j):
                inverse_deviation(norm_no(st, j))
                if st.layer == FFN:
                    inverse_deviation(norm_no(st, j) + 1)
                if st.layer != SELF:
                    wait(pool, s_xn, st.pair(j) * 2 + 2)
                    res = x_sb if st.layer == CROSS else y_sb
                    row = rows[:, 1 if st.layer == CROSS else 3, :]
                    for s in range(2):
                        r = res[:, st.first + (2 * j + s), :]
                        last = nc.gpsimd.tensor_tensor(r, r, row, ALU.add)
                    last.then_inc(s_resbias, 1)

            def low_parts(st, j):
                i = j % 2
                n = 1 if st.layer == SELF else 2
                wait(pool, s_mid, st.pair(j) + 1)
                nc.gpsimd.tensor_tensor(parts[:, i, 2, 0:n, :], rest[:, 0:n, :], parts[:, i, 1, 0:n, :],
                                        ALU.subtract).then_inc(s_lo, 1)

            def self_values(st, j):
                wait(pool, s_xn, st.pair(j) * 2 + 2)
                for s in range(2):
                    wait(pool, s_pv, (st.pair(j) * 2 - 2) * NG + PV_CREDIT, s_apart_pool)
                    nc.gpsimd.tensor_copy(vaug[:, (2 * j + s) % UNROLL, :, 0:HD],
                                          xn[:, j % 2, s, :].rearrange("p (d h) -> p h d", d=HD)).then_inc(s_v, 1)

            z = Step(pool, SELF, 0)
            start_pair(z, 0)
            low_parts(z, 0)
            pool.wait_ge(s_dve_const, 1)
            start_pair(z, 1)
            self_values(z, 0)
            low_parts(z, 1)
            constants_of_layers()
            pool.wait_ge(s_w, 16 * 15)

            def last_norm(pair):
                inverse_deviation(pair + 4 * NPAIR)
                two = slice(2 * pair, 2 * pair + 2)
                nc.gpsimd.tensor_tensor(rows_out[:, two, D:2 * D], x_sb[:, two, :], y_sb[:, two, :],
                                        ALU.add).then_inc(s_rr, 1)

            def slot(st, k, last):
                j = k // 2
                pair_after = ahead(pool, st, j + 2, last, 2)
                early, late = last_norms(st, k, last)
                if early and k == 0:
                    pool.wait_ge(s_e, 2 * B * NG)
                    nc.gpsimd.iota(rows_out.bitcast(i32)[:, :, 2 * D], pattern=[[S, B]], base=0,
                                   channel_multiplier=1).then_inc(s_rr, 1)
                for pair in early + late:
                    last_norm(pair)
                if k % 2 == 0 and pair_after:
                    start_pair(*pair_after)
                if k % 2 == 1:
                    if st.layer == SELF and not (last and j == 1):
                        self_values(st, j + 1)
                    if pair_after:
                        low_parts(*pair_after)

            for layer in (SELF, CROSS, FFN):
                steps(pool, layer, slot)

            last_norm(LEFT)

            pool.wait_ge(s_fill, 16)
            pool.wait_ge(s_rr, NPAIR + 1)
            pool.wait_ge(s_copied, NPAIR)
            pool.wait_ge(s_route, 1)
            for n in range(B):
                nc.gpsimd.indirect_dma_start(
                    out=routed, out_offset=bass.IndirectOffsetOnAxis(ap=position_i[:, n:n + 1], axis=0),
                    in_=rows_out[:, n, :], in_offset=None).then_inc(s_routed, 16)

            def store_tile(i, buf):
                wait(pool, s_sum, i + (1 + SUM_CREDIT), s_apart_pool)
                nc.gpsimd.indirect_dma_start(
                    out=out.rearrange("b s d -> (b s) d"),
                    out_offset=bass.IndirectOffsetOnAxis(ap=tile_res[:, buf, :].bitcast(i32)[:, D:D + 1], axis=0),
                    in_=tile_res[:, buf, 0:D], in_offset=None,
                    bounds_check=B * S - 1, oob_is_err=False).then_inc(s_stored[buf], 16)

            with pool.Fori(0, NTILES // TBUF) as t:
                for k in range(TBUF):
                    store_tile(t * TBUF + k, k)
            for i in range(NTILES // TBUF * TBUF, NTILES):
                store_tile(i, i % TBUF)

        @block.tensor
        def _(pe):
            def mm(o, lhsT, rhs, start=True, stop=True, **kw):
                return nc.tensor.matmul(o, lhsT, rhs, start=start, stop=stop, **kw)

            def tr(o, src, stop=True):
                return nc.tensor.matmul(o, src, ident[:], start=True, stop=stop, is_transpose=True)

            def transposes(st, j):
                i = j % 2
                wait(pe, s_xn, st.pair(j) * 2 + 2)
                if st.layer == SELF:
                    wait(pe, s_r1, st.pair(j))
                elif st.layer == CROSS:
                    wait(pe, s_ctx[i], st.t * 16 + (j // 2 * 16 + 16))
                for s in range(2):
                    last = tr(pb[:, s * S:(s + 1) * S], xn[:, i, s, :])
                if st.layer == CROSS:
                    for s in range(2):
                        last = tr(pb[:, PAIR + s * S:PAIR + (s + 1) * S], ctx_in[:, i, s, :])
                last.then_inc(s_t, 1)

            def qk_products(st, j):
                i, key_side = j % 2, 1 if st.layer == CROSS else 0
                wq, wk = ("xq", "xk") if st.layer == CROSS else ("fq", "fk")
                wait(pe, s_hT, st.pair(j) + 1 - NPAIR)
                mm(pb[:, 0:PAIR], wx[wq][:], hT[:, i, 0, :])
                mm(pb[:, PAIR:2 * PAIR], wx[wk][:], hT[:, i, key_side, :]).then_inc(s_qkp, 1)

            def v_products(st, j):
                i, key_side = j % 2, 1 if st.layer == CROSS else 0
                wv = wx["xv" if st.layer == CROSS else "fv"]
                for s in range(2):
                    last = mm(pb[:, s * S:(s + 1) * S], hT[:, i, key_side, s * S:(s + 1) * S], wv[:])
                last.then_inc(s_vp, 1)

            def score_maxes(st, k, g):
                wait(pe, s_mfree, st.maxuse(k, g) + (1 - 2 + MFREE_CREDIT))
                if g == 0:
                    wait(pe, s_stack[k // 2 % 2], st.turn(k // 2) * READS + READS)
                i, s, bank = k // 2 % 2, k % 2, mbk[(k * PERM_M + g) % 2]
                for h in range(G):
                    last = mm(bank[:, h * S:(h + 1) * S],
                              stack[:, i, 0, g * G + h, s * S:(s + 1) * S], stack[:, i, 1, g * G + h, s * S:(s + 1) * S])
                last.then_inc(s_mp, 1)

            def max_transposed(st, k):
                wait(pe, s_mparts, st.batch(k) + (1 - B))
                wait(pe, s_mfree, st.maxuse(k, NG) + (1 - 2 + MFREE_CREDIT))
                bank = mbk[(k * PERM_M + NG) % 2]
                nc.tensor.transpose(bank[:].bitcast(bf16)[:, 0:128], maxparts[:], identb[:]).then_inc(s_mp, 1)

            def scores(st, k, g):
                i, s, bank = k // 2 % 2, k % 2, sbk[g % 2]
                wait(pe, s_p, st.group(k, g) + (1 - 2 + P_CREDIT))
                if g == 0:
                    wait(pe, s_stack[i], st.turn(k // 2) * READS + READS)
                    if st.layer == CROSS:
                        wait(pe, s_bias[k % 4], (st.t + k // 4) * 32 + 32)
                    if st.layer != SELF:
                        wait(pe, s_mfree, st.maxuse(k, NG) + (1 + MFREE_CREDIT))
                for h in range(G):
                    o, head = bank[:, h * S:(h + 1) * S], g * G + h
                    q = stack[:, i, 0, head, s * S:(s + 1) * S]
                    key = stack[:, i, 1, head, s * S:(s + 1) * S]
                    if st.layer == SELF:
                        mm(o, identb[:], causal[:], stop=False)
                    elif st.layer == CROSS:
                        tr(o, bias_in[:, k % 4, head, :], stop=False)
                    last = mm(o, key, q, start=st.layer == FFN, stop=st.layer == SELF)
                    if st.layer != SELF:
                        last = mm(o, pick[:, head, :], maxT[:, k % 2, :], start=False)
                last.then_inc(s_e, 1)

            def add_outputs(st, k, g):
                wait(pe, s_p, st.group(k, g) + (1 + P_CREDIT))
                if g == 0:
                    wait(pe, s_v, st.batch(k) + (2 - k % 2))
                    wait(pe, s_oevac, st.batch(k) + (1 - 2 + OEV_CREDIT))
                for h in range(G):
                    last = mm(obk[k % 2][VC * h:VC * (h + 1), g * S:(g + 1) * S], vaug[:, k, g * G + h, :],
                              probs[:, g, h * S:(h + 1) * S], tile_position=(0, VC * h))
                last.then_inc(s_pv, 1)

            def out_transposed(st, k):
                wait(pe, s_oevac, st.batch(k) + (1 + OEV_CREDIT))
                wait(pe, s_res, st.batch(k) + (1 - 1 + RES_CREDIT))
                for g in range(NG):
                    last = tr(fb[:, g * S:(g + 1) * S], outT[:, k % 2, g * S:(g + 1) * S])
                last.then_inc(s_otr, 1)

            def attention_transposed(st, k):
                wait(pe, s_att, st.batch(k) + 1)
                tr(fb[:, 0:S], att[:]).then_inc(s_atr, 1)

            def out_projected(st, k):
                if st.layer == CROSS:
                    wait(pe, s_att, st.batch(k) + 1)
                    for d in range(HD):
                        last = mm(fb[:, 0:D], att_sel[:, d, :, :].rearrange("p h t -> p (h t)"), wxo[:, d, :],
                                  start=d == 0, stop=d == HD - 1)
                    last.then_inc(s_oproj, 1)
                else:
                    wait(pe, s_attT, st.batch(k) + (1 - 2 * B))
                    mm(fb[:, 0:D], attT[:], wx["fo"][:]).then_inc(s_oproj, 1)

            pe.sem_inc(s_pv, PV_CREDIT)
            pe.sem_inc(s_otr, OTR_CREDIT)
            pe.sem_inc(s_dn, DN_CREDIT)
            pe.wait_ge(s_ident, 6)
            def next_transposes(st, k, last):
                j = k // 2
                if st.layer != SELF:
                    wait(pe, s_v, st.batch(2 * (j + 1)))
                elif last and j == 0:
                    wait(pe, s_r1, NPAIR)
                elif last:
                    wait(pe, s_qk, 1)
                transposes(*ahead(pe, st, j + 2, last, 2))

            def last_norm(pair):
                pe.wait_ge(s_xn, 2 * (3 * NPAIR + pair) + 2)
                for s in range(2):
                    last = tr(pb[:, s * S:(s + 1) * S], xn[:, pair % 2, s, :])
                last.then_inc(s_t, 1)

            def gate(pair):
                pe.wait_ge(s_hn2, pair + 1)
                for n in (2 * pair, 2 * pair + 1):
                    last = mm(pb[:, PAIR + n * E:PAIR + (n + 1) * E], hn2T[:, n * S:(n + 1) * S], gate_w[:])
                last.then_inc(s_g, 1)

            z = Step(pe, SELF, 0)
            transposes(z, 0)
            transposes(z, 1)
            pe.wait_ge(s_dve_const, 2)
            scores(z, 0, 0)
            scores(z, 0, 1)
            pe.wait_ge(s_pool_const, 8)
            pe.wait_ge(s_dve_const, 4)
            pe.wait_ge(s_w, 16 * 15)

            def slot(st, k, last):
                j = k // 2
                full = st.layer != SELF
                batch_next, batch_after = ahead(pe, st, k + 1, last, UNROLL), ahead(pe, st, k + 2, last, UNROLL)
                pair_next, pair_after = ahead(pe, st, j + 1, last, 2), ahead(pe, st, j + 2, last, 2)
                maxes_next = batch_next and batch_next[0].layer != SELF
                maxes_after = batch_after and batch_after[0].layer != SELF
                add_outputs(st, k, 0)
                if maxes_next:
                    score_maxes(*batch_next, 3)
                scores(st, k, 2)
                add_outputs(st, k, 1)
                scores(st, k, 3)
                if maxes_next:
                    max_transposed(*batch_next)
                add_outputs(st, k, 2)
                if batch_next:
                    scores(*batch_next, 0)
                add_outputs(st, k, 3)
                if batch_next and (st.layer != CROSS or k % 2 == 0):
                    scores(*batch_next, 1)
                if maxes_after and k % 2 == 1:
                    score_maxes(*batch_after, 0)
                early_norm, late_norm = last_norms(st, k, last)
                for pair in early_norm:
                    if pair == 0:
                        pe.wait_ge(s_v, 2 * (3 * NPAIR - 1))
                    elif k >= 2:
                        pe.wait_ge(s_v, 2 * 3 * NPAIR)
                    if pair > 0:
                        gate(pair - 1)
                    last_norm(pair)
                out_transposed(st, k)
                early = st.layer == CROSS and pair_after[0].layer == CROSS
                if k % 2 == 0 and early:
                    next_transposes(st, k, last)
                if st.layer == CROSS and k % 2 == 1:
                    scores(*batch_next, 1)
                if maxes_after and k % 2 == 0:
                    score_maxes(*batch_after, 0)
                if maxes_after:
                    score_maxes(*batch_after, 1)
                if k % 2 == 0 and pair_after and not early:
                    next_transposes(st, k, last)
                if k % 2 == 0 and early:
                    qk_products(*pair_after)
                if k % 2 == 1 and pair_next and pair_next[0].layer != SELF:
                    held = pair_after or pair_next
                    wait(pe, s_qk, held[0].pair(held[1]) + (1 - NPAIR))
                    for pair in early_norm:
                        pe.wait_ge(s_hn2, pair + 1)
                    v_products(*pair_next)
                if st.layer == FFN:
                    attention_transposed(st, k)
                outputs_first = st.layer == CROSS and k % 2 == 0
                if maxes_after and not outputs_first:
                    score_maxes(*batch_after, 2)
                if k % 2 == 0 and not early and pair_after and pair_after[0].layer != SELF:
                    qk_products(*pair_after)
                if full:
                    out_projected(st, k)
                if outputs_first:
                    score_maxes(*batch_after, 2)
                for pair in late_norm:
                    gate(pair - 1)
                    last_norm(pair)

            for layer in (SELF, CROSS, FFN):
                steps(pe, layer, slot)

            gate(LEFT - 1)
            last_norm(LEFT)
            gate(LEFT)

            pe.wait_ge(s_onehot, 1)
            mm(fb[:, 0:B * E], before[:], onehot[:].rearrange("p b e -> p (b e)"))
            mm(fb[:, B * E:2 * B * E], ones[:], onehot[:].rearrange("p b e -> p (b e)")).then_inc(s_rank, 1)

            def expert(i):
                return pe.value_load(tile_expert_i[0:1, i:i + 1] if isinstance(i, int)
                                     else tile_expert_i[0:1, bass.ds(i, 1)], min_val=0, max_val=E - 1)

            def tile_transposed(i, k):
                wait(pe, s_values[k % TBUF], (i - k % TBUF) * (16 // TBUF) + 16)
                wait(pe, s_tT, i - 1)
                tr((pb, fb)[k % 2][:, 0:S], tile_xn[:, k % TBUF, :]).then_inc(s_xT, 1)

            def hidden(i, k):
                e = expert(i)
                wait(pe, s_tT, i + 1)
                wait(pe, s_mid2, i - 1)
                mm(sbk[k % 2][:], hn2T_tile[:, k % 2, :],
                   w1[:, bass.ds(e, 1), :].rearrange("p o f -> p (o f)")).then_inc(s_up, 1)

            def hidden_transposed(i, k):
                wait(pe, s_mid2, i + 1)
                wait(pe, s_midT, i + (1 - 2 + MIDT_CREDIT))
                for c in range(FC):
                    last = tr(mbk[k % 2][:, c * S:(c + 1) * S], mid[:, k % 2, c * 128:(c + 1) * 128])
                last.then_inc(s_midp, 1)

            def expert_output(i, k):
                e = expert(i)
                wait(pe, s_midT, i + (1 + MIDT_CREDIT))
                wait(pe, s_moe_out, i + (1 - 2 + SUM_CREDIT))
                for c in range(FC):
                    last = mm(obk[k % 2][:, 0:D], midT[:, k % 2, c * S:(c + 1) * S],
                              w2[:, bass.ds(e, 1), c, :].rearrange("p o d -> p (o d)"), start=c == 0, stop=c == FC - 1)
                last.then_inc(s_dn, 1)

            pe.wait_ge(s_moe, 64)
            pe.wait_ge(s_route, 1)
            tile_transposed(0, 0)
            tile_transposed(1, 1)
            hidden(0, 0)

            def expert_slot(s, k):
                if due(s, 1):
                    hidden(s + 1, k + 1)
                if due(s, 0):
                    hidden_transposed(s, k)
                if due(s, 2):
                    tile_transposed(s + 2, k + 2)
                if due(s, -1):
                    expert_output(s - 1, k - 1)

            tile_slots(pe, expert_slot)

        @block.scalar
        def _(act):
            def take_hT(st, j):
                i = j % 2
                wait(act, s_t, st.pair(j) + 1)
                wait(act, s_vp, st.pair(j) - NPAIR - 1)
                if st.layer == CROSS:
                    nc.scalar.copy(hT[:, i, :, :].rearrange("p a k -> p (a k)"), pb[:]).then_inc(s_hT, 1)
                else:
                    nc.scalar.activation(hT[:, i, 0, :], pb[:, 0:PAIR], ACT.Identity,
                                         bias=cols[:, 5:6], scale=cols[:, 4:5]).then_inc(s_hT, 1)

            def take_qk(st, j):
                wait(act, s_qkp, st.pair(j) + 1 - NPAIR)
                wait(act, s_r1, st.pair(j))
                if st.layer == CROSS:
                    nc.scalar.activation(qk[:, 0, :], pb[:, 0:PAIR], ACT.Identity, bias=xbq_scaled[:], scale=SCALE)
                    nc.scalar.activation(qk[:, 1, :], pb[:, PAIR:2 * PAIR], ACT.Identity,
                                         bias=cols[:, 1:2], scale=1.0).then_inc(s_qk, 1)
                else:
                    nc.scalar.activation(qk[:, 0, :], pb[:, 0:PAIR], ACT.Identity, bias=cols[:, 2:3], scale=1.0)
                    nc.scalar.activation(qk[:, 1, :], pb[:, PAIR:2 * PAIR], ACT.Identity,
                                         bias=cols[:, 3:4], scale=1.0).then_inc(s_qk, 1)

            def high_parts(st, j):
                i = j % 2
                wait(act, s_wr[i], st.turn(j) * WRITES)
                if st.layer == SELF:
                    wait(act, s_t, st.pair(j) + 1)
                    nc.scalar.copy(parts[:, i, 0, 0, :], pb[:, 0:PAIR]).then_inc(s_hi, 1)
                else:
                    wait(act, s_qk, st.pair(j) + 1 - NPAIR)
                    nc.scalar.copy(parts[:, i, 0, :, :], qk[:]).then_inc(s_hi, 1)

            def middle_parts(st, j):
                i, n = j % 2, 1 if st.layer == SELF else 2
                wait(act, s_r1, st.pair(j) + 1)
                nc.scalar.copy(parts[:, i, 1, 0:n, :], rest[:, 0:n, :]).then_inc(s_mid, 1)

            def exponentials(st, k, g):
                wait(act, s_e, st.group(k, g) + 1)
                wait(act, s_pv, st.group(k, g) + (1 - 4 + PV_CREDIT))
                nc.scalar.activation(probs[:, g, :], sbk[g % 2][:], ACT.Exp,
                                     scale=1.0 if st.layer == CROSS else SCALE).then_inc(s_p, 1)

            def take_out(st, k):
                wait(act, s_pv, st.group(k, NG) + PV_CREDIT)
                wait(act, s_otr, st.batch(k) + (1 - 2 + OTR_CREDIT))
                nc.scalar.copy(outT[:, k % 2, :], obk[k % 2][:]).then_inc(s_oevac, 1)

            def take_attT(st, k):
                wait(act, s_atr, st.batch(k) + (1 - 2 * B))
                nc.scalar.copy(attT[:], fb[:, 0:S]).then_inc(s_attT, 1)

            act.sem_inc(s_p, P_CREDIT)
            act.sem_inc(s_oevac, OEV_CREDIT)
            act.sem_inc(s_midT, MIDT_CREDIT)
            act.wait_ge(s_ident, 4)
            nc.scalar.copy(stack_tail(0),
                           zero[64:KROWS, :].to_broadcast([KROWS - 64, NH * PAIR])).then_inc(s_zero[0], 1)
            z = Step(act, SELF, 0)
            for j in range(2):
                high_parts(z, j)
                middle_parts(z, j)
            for g in range(NG // 2):
                exponentials(z, 0, g)
            act.wait_ge(s_w, 16 * 15)
            act.wait_ge(s_dve_const, 5)

            def last_norm(pair):
                i = pair % 2
                act.wait_ge(s_xn, 2 * (3 * NPAIR + pair) + 2)
                nc.scalar.copy(rows_out[:, 2 * pair:2 * pair + 2, 0:D], xn[:, i, :, :]).then_inc(s_copied, 1)
                act.wait_ge(s_t, pair + (3 * NPAIR + 1))
                nc.scalar.activation(hn2T[:, pair * PAIR:(pair + 1) * PAIR], pb[:, 0:PAIR], ACT.Identity,
                                     bias=cols[:, 7:8], scale=cols[:, 6:7]).then_inc(s_hn2, 1)

            def slot(st, k, last):
                batch_next = ahead(act, st, k + 1, last, UNROLL)
                pair_after = ahead(act, st, k // 2 + 2, last, 2)
                exponentials(st, k, 2)
                exponentials(st, k, 3)
                if k % 2 == 1 and pair_after:
                    middle_parts(*pair_after)
                if batch_next:
                    exponentials(*batch_next, 0)
                take_out(st, k)
                if batch_next:
                    exponentials(*batch_next, 1)
                if k % 2 == 0 and pair_after:
                    if pair_after[0].layer == SELF:
                        high_parts(*pair_after)
                    else:
                        take_hT(*pair_after)
                early_norm, late_norm = last_norms(st, k, last)
                for pair in early_norm:
                    if pair == 0:
                        act.wait_ge(s_e, 2 * B * NG)
                    last_norm(pair)
                if st.layer == FFN:
                    take_attT(st, k)
                for pair in late_norm:
                    last_norm(pair)
                if k % 2 == 0 and pair_after and pair_after[0].layer != SELF:
                    take_qk(*pair_after)
                    high_parts(*pair_after)

            for layer in (SELF, CROSS, FFN):
                steps(act, layer, slot)

            last_norm(LEFT)

            def take_tile(i, k):
                act.wait_ge(s_xT, i + 1)
                wait(act, s_up, i - 1)
                nc.scalar.activation(hn2T_tile[:, k % 2, :], (pb, fb)[k % 2][:, 0:S], ACT.Identity,
                                     bias=cols[:, 7:8], scale=cols[:, 6:7]).then_inc(s_tT, 1)

            def rectify(i, k):
                act.wait_ge(s_midp, i + 1)
                wait(act, s_dn, i + (1 - 2 + DN_CREDIT))
                nc.scalar.activation(midT[:, k % 2, :], mbk[k % 2][:], ACT.Relu).then_inc(s_midT, 1)

            take_tile(0, 0)
            take_tile(1, 1)

            def expert_slot(s, k):
                if due(s, 0):
                    rectify(s, k)
                if due(s, 2):
                    take_tile(s + 2, k + 2)

            tile_slots(act, expert_slot)

        @block.vector
        def _(dve):
            dve.sem_inc(s_res, RES_CREDIT)
            dve.sem_inc(s_mfree, MFREE_CREDIT)
            dve.sem_inc(s_moe_out, SUM_CREDIT)
            dve.sem_inc(s_sum, SUM_CREDIT)
            nc.vector.memset(vaug[:], 0.0).then_inc(s_chain, 1)
            dve.wait_ge(s_chain, 1)
            nc.vector.memset(vaug[:, :, :, HD:HD + 1], 1.0).then_inc(s_dve_const, 1)
            dve.wait_ge(s_x[0], 16)

            def norm_no(st, j):
                return st.pair(j) if st.layer < FFN else (st.t * 4 + (2 * NPAIR + 2 * j))

            def row_stats(src, no):
                wait(dve, s_rstd, no, s_apart_dve)
                for s in range(2):
                    last = nc.vector.bn_stats(stats[:, s, :], src(s))
                last.then_inc(s_stats, 1)
                wait(dve, s_stats, no + 1, s_apart_dve)
                for s in range(2):
                    nc.vector.bn_aggr(meanvar[:, s, :], stats[:, s, :]).then_inc(s_mv, 1)

            def normalise(dst, src, no, sem_done):
                wait(dve, s_mv, no * 2 + 2)
                wait(dve, s_rstd, no + 1)
                for s in range(2):
                    nc.vector.tensor_scalar(dst(s), src(s), meanvar[:, s, 0:1], rstd[:, s:s + 1],
                                            ALU.subtract, ALU.mult).then_inc(sem_done, 1)

            def x_rows(st, j):
                return lambda s: x_sb[:, st.first + (2 * j + s), :]

            def y_rows(st, j):
                return lambda s: y_sb[:, st.first + (2 * j + s), :]

            def xn_rows(j, layer=FFN):
                if layer == SELF:
                    return lambda s: xn[:, j % 2, s, :].rearrange("p (d h) -> p h d", d=HD)
                return lambda s: xn[:, j % 2, s, :]

            def norm_stats(st, j):
                if st.layer != SELF and isinstance(st.t, int) and j < 2:
                    wait(dve, s_res, B * (st.layer - 1) + (2 * j + 2 + RES_CREDIT))
                row_stats(x_rows(st, j), norm_no(st, j))

            def norm_between(st, j):
                if st.layer == FFN:
                    no = norm_no(st, j)
                    normalise(y_rows(st, j), x_rows(st, j), no, s_y)
                    wait(dve, s_y, st.first + (2 * j + 2))
                    row_stats(y_rows(st, j), no + 1)

            def norm_rows(st, j):
                no = norm_no(st, j) + (1 if st.layer == FFN else 0)
                src = y_rows(st, j) if st.layer == FFN else x_rows(st, j)
                wait(dve, s_t, st.pair(j) - 1)
                if st.layer == SELF or st.layer == CROSS and isinstance(st.t, int) and j < 2:
                    wait(dve, s_v, (st.pair(j) - 1) * 2)
                if st.layer == SELF:
                    rows_in = src
                    src = lambda s: rows_in(s).rearrange("p (h d) -> p h d", d=HD)
                normalise(xn_rows(j, st.layer), src, no, s_xn)

            def first_rest(st, j):
                i = j % 2
                wait(dve, s_hi, st.pair(j) + 1)
                wait(dve, s_lo, st.pair(j))
                if st.layer == SELF:
                    nc.vector.tensor_tensor(rest[:, 0, :], pb[:, 0:PAIR], parts[:, i, 0, 0, :],
                                            ALU.subtract).then_inc(s_r1, 1)
                else:
                    nc.vector.tensor_tensor(rest[:], qk[:], parts[:, i, 0, :, :], ALU.subtract).then_inc(s_r1, 1)

            def take_values(st, j):
                wait(dve, s_vp, st.pair(j) + 1 - NPAIR)
                wait(dve, s_pv, (st.pair(j) * 2 - 2) * NG + PV_CREDIT)
                row = rows[:, 0 if st.layer == CROSS else 2, :]
                for s in range(2):
                    nc.vector.tensor_tensor(vaug[:, (2 * j + s) % UNROLL, :, 0:HD],
                                            pb[:, s * S:(s + 1) * S].rearrange("p (h d) -> p h d", d=HD),
                                            row.rearrange("p (h d) -> p h d", d=HD), ALU.add).then_inc(s_v, 1)

            def row_maxes(st, k, g):
                bank = mbk[(k * PERM_M + g) % 2]
                if st.layer == CROSS and g == 0:
                    wait(dve, s_bias[k % 4], (st.t + k // 4) * 32 + 32)
                wait(dve, s_mp, st.maxuse(k, g) + 1, s_apart_dve)
                if st.layer == CROSS:
                    for h in range(G):
                        head = g * G + h
                        last = nc.vector.tensor_tensor_reduce(
                            out=bank[:, h * S:(h + 1) * S], in0=bank[:, h * S:(h + 1) * S],
                            in1=bias_in[:, k % 4, head, :], scale=1.0,
                            scalar=-3.0e38, op0=ALU.add, op1=ALU.max, accum_out=rowmax[:, head:head + 1])
                else:
                    last = nc.vector.tensor_reduce(rowmax[:, g * G:(g + 1) * G],
                                                   bank[:].rearrange("p (h k) -> p h k", h=G), AX.X, ALU.max)
                last.then_inc(s_mfree, 1)

            def max_parts(st, k):
                wait(dve, s_mfree, st.maxuse(k, NG) + MFREE_CREDIT)
                nc.vector.tensor_scalar(maxparts[:, 0:NH], rowmax[:], -1.0, None, ALU.mult).then_inc(s_mhi, 1)
                wait(dve, s_mhi, st.batch(k) + (1 - B))
                nc.vector.scalar_tensor_tensor(out=maxparts[:, NH:2 * NH], in0=rowmax[:], scalar=-1.0,
                                               in1=maxparts[:, 0:NH], op0=ALU.mult,
                                               op1=ALU.subtract).then_inc(s_mparts, 1)

            def take_maxT(st, k):
                wait(dve, s_mp, st.maxuse(k, NG) + 1)
                wait(dve, s_e, (st.batch(k) - 1) * NG)
                nc.vector.tensor_copy(maxT[:, k % 2, :],
                                      mbk[(k * PERM_M + NG) % 2][:].bitcast(bf16)[:, 0:128]).then_inc(s_mfree, 1)

            def attention(st, k):
                wait(dve, s_otr, st.batch(k) + (1 + OTR_CREDIT))
                o = fb[:].rearrange("p (h c) -> p h c", c=VC)
                nc.vector.reciprocal(rowsum_inv[:], o[:, :, HD]).then_inc(s_inv, 1)
                wait(dve, s_inv, st.batch(k) + 1)
                if st.layer == CROSS:
                    nc.vector.tensor_tensor(inv_sel[:], rowsum_inv[:].unsqueeze(2).to_broadcast([128, NH, TQ]),
                                            in_block[:].unsqueeze(1).to_broadcast([128, NH, TQ]),
                                            ALU.mult).then_inc(s_invsel, 1)
                    wait(dve, s_invsel, st.batch(k) + (1 - B))
                    nc.vector.tensor_tensor(
                        att_sel[:], o[:, :, 0:HD].rearrange("p h d -> p d h").unsqueeze(3).to_broadcast([128, HD, NH, TQ]),
                        inv_sel[:].unsqueeze(1).to_broadcast([128, HD, NH, TQ]), ALU.mult).then_inc(s_att, 1)
                    return
                nc.vector.tensor_tensor(att[:].rearrange("p (h d) -> p h d", d=HD), o[:, :, 0:HD],
                                        rowsum_inv[:].unsqueeze(2).to_broadcast([128, NH, HD]),
                                        ALU.mult).then_inc(s_att, 1)
                if st.layer == SELF:
                    wait(dve, s_att, st.batch(k) + 1)
                    r = x_sb[:, st.first + k, :]
                    nc.vector.tensor_tensor(r, r, att[:], ALU.add).then_inc(s_res, 1)

            def residual(st, k):
                res = x_sb if st.layer == CROSS else y_sb
                if k % 2 == 0:
                    wait(dve, s_resbias, st.pair(k // 2) + (1 - NPAIR))
                wait(dve, s_oproj, st.batch(k) + (1 - B))
                r = res[:, st.first + k, :]
                nc.vector.tensor_tensor(r, fb[:, 0:D], r, ALU.add).then_inc(s_res, 1)

            z = Step(dve, SELF, 0)
            norm_stats(z, 0)
            norm_rows(z, 0)
            first_rest(z, 0)
            norm_stats(z, 1)
            dve.wait_ge(s_ident, 6)
            nc.vector.tensor_copy(identb[:], ident[:]).then_inc(s_dve_const, 1)
            norm_rows(z, 1)
            first_rest(z, 1)
            nc.vector.memset(stack_tail(1), 0.0).then_inc(s_zero[1], 1)
            dve.wait_ge(s_w, 16 * 15)
            nc.vector.tensor_scalar(xbq_scaled[:], cols[:, 0:1], SCALE, None, ALU.mult).then_inc(s_dve_const, 1)
            nc.vector.memset(maxparts[:], 0.0).then_inc(s_dve_const, 1)
            nc.vector.memset(ones[:], 1.0).then_inc(s_dve_const, 1)
            nc.vector.memset(prefix[:], 0.0).then_inc(s_chain, 1)
            nc.vector.memset(starts[:], 0.0).then_inc(s_chain, 1)
            dve.wait_ge(s_x[1], 16)
            dve.wait_ge(s_pool_const, 13)

            def last_stats(pair):
                dve.wait_ge(s_res, 2 * B + 2 * pair + (2 + RES_CREDIT))
                row_stats(lambda s: y_sb[:, 2 * pair + s, :], 4 * NPAIR + pair)

            def last_rows(pair):
                dve.wait_ge(s_t, 3 * NPAIR + pair - 1)
                wait(dve, s_copied, pair - 1)
                normalise(xn_rows(pair), lambda s: y_sb[:, 2 * pair + s, :], 4 * NPAIR + pair, s_xn)

            def slot(st, k, last):
                j = k // 2
                batch_next, batch_after = ahead(dve, st, k + 1, last, UNROLL), ahead(dve, st, k + 2, last, UNROLL)
                pair_next, pair_after = ahead(dve, st, j + 1, last, 2), ahead(dve, st, j + 2, last, 2)
                maxes_next = batch_next and batch_next[0].layer != SELF
                maxes_after = batch_after and batch_after[0].layer != SELF
                normalised = pair_after if k % 2 == 0 else None
                if normalised and normalised[0].layer == FFN:
                    norm_stats(*normalised)
                if maxes_next:
                    row_maxes(*batch_next, 3)
                    max_parts(*batch_next)
                if k % 2 == 1 and pair_after:
                    first_rest(*pair_after)
                if maxes_next:
                    take_maxT(*batch_next)
                if normalised and normalised[0].layer != FFN:
                    norm_stats(*normalised)
                if normalised:
                    norm_between(*normalised)
                    if st.layer != FFN:
                        norm_rows(*normalised)
                early_norm, late_norm = last_norms(st, k, last)
                for pair in early_norm:
                    last_stats(pair)
                if maxes_after and k % 2 == 1:
                    row_maxes(*batch_after, 0)
                for pair in early_norm:
                    last_rows(pair)
                for pair in late_norm:
                    last_stats(pair)
                attention(st, k)
                for pair in late_norm:
                    last_rows(pair)
                if normalised and st.layer == FFN:
                    norm_rows(*normalised)
                if maxes_after and k % 2 == 0:
                    row_maxes(*batch_after, 0)
                if maxes_after:
                    row_maxes(*batch_after, 1)
                if k % 2 == 1 and pair_next and pair_next[0].layer != SELF:
                    take_values(*pair_next)
                if maxes_after:
                    row_maxes(*batch_after, 2)
                if st.layer != SELF:
                    residual(st, k)

            for layer in (SELF, CROSS, FFN):
                if layer != SELF:
                    wait(dve, s_res, B * layer + RES_CREDIT)
                steps(dve, layer, slot)

            last_stats(LEFT)
            last_rows(LEFT)

            chain = [3]

            def link(ins):
                chain[0] += 1
                ins.then_inc(s_chain, 1)
                dve.wait_ge(s_chain, chain[0])

            over_b = lambda t: t.unsqueeze(1).to_broadcast([128, B, E])
            over_e = lambda t: t.unsqueeze(2).to_broadcast([128, B, E])
            dve.wait_ge(s_g, NPAIR)
            link(nc.vector.tensor_tensor(logits[:], pb[:, PAIR:PAIR + B * E].rearrange("p (b e) -> p b e", e=E),
                                         over_b(gate_b[:]), ALU.add))
            link(nc.vector.tensor_reduce(best[:], logits[:], AX.X, ALU.max))
            link(nc.vector.tensor_tensor(is_best[:], logits[:], over_e(best[:]), ALU.is_equal))
            link(nc.vector.scalar_tensor_tensor(out=place[:], in0=is_best[:], scalar=-float(E), in1=over_b(expert_no[:]),
                                                op0=ALU.mult, op1=ALU.add))
            link(nc.vector.tensor_reduce(first_best[:], place[:], AX.X, ALU.min))
            nc.vector.scalar_tensor_tensor(
                out=onehot[:], in0=over_e(first_best[:]), scalar=float(E), in1=over_b(expert_no[:]),
                op0=ALU.add, op1=ALU.is_equal).then_inc(s_onehot, 1)

            dve.wait_ge(s_rank, 1)
            half_b, half_e = B // 2, E // 2
            link(nc.vector.tensor_copy(prefix[:, 0, half_b:, :],
                                       fb[:, B * E:2 * B * E].rearrange("p (b e) -> p b e", e=E)))
            i, step = 0, 1
            while step < B:
                link(nc.vector.tensor_tensor(prefix[:, 1 - i, half_b:, :], prefix[:, i, half_b:, :],
                                             prefix[:, i, half_b - step:half_b - step + B, :], ALU.add))
                i, step = 1 - i, step * 2
            link(nc.vector.tensor_tensor(over_end[:], prefix[:, i, half_b + B - 1, :].unsqueeze(2).to_broadcast([128, E, B]),
                                         tile_ends[:].unsqueeze(1).to_broadcast([128, E, B]), ALU.is_gt))
            link(nc.vector.tensor_reduce(starts[:, 0, half_e:], over_end[:], AX.X, ALU.add))
            j, step = 0, 1
            while step < E:
                link(nc.vector.tensor_tensor(starts[:, 1 - j, half_e:], starts[:, j, half_e:],
                                             starts[:, j, half_e - step:half_e - step + E], ALU.add))
                j, step = 1 - j, step * 2
            start = starts[:, j, half_e - 1:half_e - 1 + E]
            link(nc.vector.tensor_tensor(place_in[:], fb[:, 0:B * E].rearrange("p (b e) -> p b e", e=E),
                                         prefix[:, i, half_b - 1:half_b - 1 + B, :], ALU.add))
            link(nc.vector.scalar_tensor_tensor(out=place[:], in0=over_b(start), scalar=float(TILE), in1=place_in[:],
                                                op0=ALU.mult, op1=ALU.add))
            link(nc.vector.tensor_tensor(place_in[:], place[:], onehot[:], ALU.mult))
            link(nc.vector.tensor_reduce(position[:], place_in[:], AX.X, ALU.add))
            link(nc.vector.tensor_copy(position_i[:], position[:]))
            link(nc.vector.tensor_tensor(started[:], tile_no[0:1, :].unsqueeze(2).to_broadcast([1, NTILES, E]),
                                         starts[0:1, j, half_e - 1:half_e - 1 + E].unsqueeze(1).to_broadcast([1, NTILES, E]),
                                         ALU.is_ge))
            link(nc.vector.tensor_reduce(tile_expert[:], started[:], AX.X, ALU.add))
            nc.vector.tensor_scalar(tile_expert_i[:], tile_expert[:], -1.0, None, ALU.add).then_inc(s_route, 1)
            dve.wait_ge(s_route, 1)
            dve.wait_ge(s_moe, 64)

            def expert(i):
                return dve.value_load(tile_expert_i[0:1, i:i + 1] if isinstance(i, int)
                                      else tile_expert_i[0:1, bass.ds(i, 1)], min_val=0, max_val=E - 1)

            def hidden_biased(i, k):
                e = expert(i)
                dve.wait_ge(s_up, i + 1)
                wait(dve, s_midp, i - 1)
                nc.vector.tensor_tensor(mid[:, k % 2, :], sbk[k % 2][:],
                                        b1_rows[:, bass.ds(e, 1), :].rearrange("p o f -> p (o f)"),
                                        ALU.add).then_inc(s_mid2, 1)

            def tile_summed(i, k):
                e = expert(i)
                dve.wait_ge(s_dn, i + (1 + DN_CREDIT))
                wait(dve, s_sum, i + (1 - 2 + SUM_CREDIT))
                nc.vector.tensor_tensor(moe[:, k % 2, :], obk[k % 2][:, 0:D],
                                        b2_rows[:, bass.ds(e, 1), :].rearrange("p o d -> p (o d)"),
                                        ALU.add).then_inc(s_moe_out, 1)
                dve.wait_ge(s_moe_out, i + (1 + SUM_CREDIT))
                dve.wait_ge(s_residuals[k % TBUF], (i - k % TBUF) * (16 // TBUF) + 16)
                r = tile_res[:, k % TBUF, 0:D]
                nc.vector.tensor_tensor(r, r, moe[:, k % 2, :], ALU.add).then_inc(s_sum, 1)

            hidden_biased(0, 0)

            def expert_slot(s, k):
                if due(s, 1):
                    hidden_biased(s + 1, k + 1)
                if due(s, -1):
                    tile_summed(s - 1, k - 1)

            tile_slots(dve, expert_slot)


def kernel(**inputs):
    import concourse.bacc as bacc
    from concourse.bass_utils import run_bass_kernel_spmd

    g = {k: np.ascontiguousarray(v) for k, v in inputs.items()}
    x_ = lambda n: g["L0_xattn_" + n]
    f_ = lambda n: g["L0_ffn_" + n]
    by_feature = lambda v: v.reshape(-1, NH, HD).swapaxes(1, 2).reshape(v.shape)
    arrays = {
        "x": g["x"], "ctx": g["ctx_1024"], "bias": g["fside_Bx16xSxS2_0"],
        "w_xq": by_feature(x_("Wq").T), "w_xk": by_feature(x_("Wk").T), "w_xv": x_("Wv").T, "w_xo": x_("Wo").T,
        "w_fq": by_feature(f_("wq")), "w_fk": by_feature(f_("wk")), "w_fv": f_("wv"), "w_fo": f_("wo"),
        "cols": np.stack([by_feature(x_("bq")), by_feature(x_("bk")), by_feature(f_("bq")), by_feature(f_("bk")),
                          f_("ln1_g"), f_("ln1_b"), f_("ln2_g"), f_("ln2_b")], axis=1),
        "xbv": x_("bv"), "xbo": x_("bo"), "fbv": f_("bv"), "fbo": f_("bo"),
        "gate_w": f_("gate_w"), "gate_b": f_("gate_b"), "w1": f_("w1"), "w2": f_("w2"),
        "b1": f_("b1"), "b2": f_("b2"),
    }
    arrays = {k: np.ascontiguousarray(v) for k, v in arrays.items()}
    nc = bacc.Bacc("TRN2", target_bir_lowering=False, num_devices=1)
    aps = {k: nc.dram_tensor("in_" + k, v.shape, mybir.dt.from_np(v.dtype), kind="ExternalInput").ap()
           for k, v in arrays.items()}
    out = nc.dram_tensor("out", (B, S, D), mybir.dt.float32, kind="ExternalOutput").ap()
    build(nc, aps, out)
    r = run_bass_kernel_spmd(nc, [{"in_" + k: v for k, v in arrays.items()}], core_ids=[0])
    return r.results[0]["out"]
```
